# Optimizing a Trainium2 kernel written in Bass

```python
import numpy as np
import jax
import jax.numpy as jnp

def _softmax(x, axis=-1):
    return jax.nn.softmax(x, axis=axis)

def _gelu(x):
    return jax.nn.gelu(x, approximate=True)

def _silu(x):
    return jax.nn.silu(x)

def _sigmoid(x):
    return jax.nn.sigmoid(x)

def _layernorm(x, axis=-1, eps=1e-05):
    m = jnp.mean(x, axis=axis, keepdims=True)
    v = jnp.var(x, axis=axis, keepdims=True)
    return (x - m) / jnp.sqrt(v + eps)

def _scatter_add(tgt, idx, src, axis=0):
    return tgt.at[idx].add(src)

def _segment_sum(src, seg, n):
    return jax.ops.segment_sum(src, seg, n)
kernel_name = 'mk_gnn_preln_d2_gnn_r32_ab3197'

def setup_inputs(seed: int=0):
    np.random.seed(seed)
    _w = jnp.asarray

    def _rec_inputs():
        import jax
        import jax.numpy as jnp
        _gk = jax.random.key(seed)
        x = -0.0002117 + 1 * jax.random.normal(jax.random.fold_in(_gk, 1), (3125, 256), jnp.float32)
        src = jax.random.randint(jax.random.fold_in(_gk, 2), (50000,), 0, 3125, jnp.int32)
        dst = jax.random.randint(jax.random.fold_in(_gk, 3), (50000,), 0, 3125, jnp.int32)
        _o = jnp.argsort(dst, stable=True)
        src = src[_o]
        dst = dst[_o]
        return (x, src, dst)
    x, src, dst = _rec_inputs()

    def _L0_gnn_setup():
        import jax, jax.numpy as jnp
        import numpy as np
        N_NODES = 3125
        key = jax.random.key(seed)
        k1, k2, k3, k4 = jax.random.split(key, 4)
        feat = jax.random.normal(k1, (N_NODES, 256), dtype=jnp.float32)
        bound = float(np.sqrt(6.0 / (256 + 256)))
        weight1 = jax.random.uniform(k2, (256, 256), dtype=jnp.float32, minval=-bound, maxval=bound)
        src = jax.random.randint(k3, (50000,), 0, N_NODES, dtype=jnp.int64)
        dst = jax.random.randint(k4, (50000,), 0, N_NODES, dtype=jnp.int64)
        return {'feat': feat, 'weight1': weight1, 'src': src, 'dst': dst}
    _L0_gnn_all = _L0_gnn_setup()
    _L0_gnn_in = {k: v for k, v in _L0_gnn_all.items() if k in ('weight1',)}
    del _L0_gnn_all

    def _L1_gnn_setup():
        import jax, jax.numpy as jnp
        import numpy as np
        BN_EPS = 1e-05
        CHANNELS = [256, 512, 1024, 512, 256]

        def _bn(h, gamma, beta):
            m = h.mean(axis=0)
            v = h.var(axis=0)
            return gamma * (h - m) * jax.lax.rsqrt(v + BN_EPS) + beta
        key = jax.random.key(seed)
        N, E = (50000, 25000)
        ks = jax.random.split(key, 16)
        inp = {'x': jax.random.normal(ks[0], (N, CHANNELS[0]), dtype=jnp.float32), 'edge_index': jax.random.randint(ks[1], (2, E), 0, N, dtype=jnp.int32), 'eps': jnp.float32(0.1)}
        for i in range(4):
            cin, cout = (CHANNELS[i], CHANNELS[i + 1])
            inp[f'W{i + 1}'] = jax.random.normal(ks[2 + 3 * i], (cin, cout), dtype=jnp.float32) * (1.0 / np.sqrt(cin))
            inp[f'b{i + 1}'] = jnp.zeros((cout,), dtype=jnp.float32)
            if i < 3:
                inp[f'g{i + 1}'] = jnp.ones((cout,), dtype=jnp.float32)
                inp[f'beta{i + 1}'] = jnp.zeros((cout,), dtype=jnp.float32)
        return inp
    _L1_gnn_all = _L1_gnn_setup()
    _L1_gnn_in = {k: v for k, v in _L1_gnn_all.items() if k in ('eps', 'W1', 'b1', 'g1', 'beta1', 'W2', 'b2', 'g2', 'beta2', 'W3', 'b3', 'g3', 'beta3', 'W4', 'b4')}
    del _L1_gnn_all
    return {'x': x, 'src': src, 'dst': dst, 'L0_gnn_weight1': _L0_gnn_in['weight1'], 'L1_gnn_eps': _L1_gnn_in['eps'], 'L1_gnn_W1': _L1_gnn_in['W1'], 'L1_gnn_b1': _L1_gnn_in['b1'], 'L1_gnn_g1': _L1_gnn_in['g1'], 'L1_gnn_beta1': _L1_gnn_in['beta1'], 'L1_gnn_W2': _L1_gnn_in['W2'], 'L1_gnn_b2': _L1_gnn_in['b2'], 'L1_gnn_g2': _L1_gnn_in['g2'], 'L1_gnn_beta2': _L1_gnn_in['beta2'], 'L1_gnn_W3': _L1_gnn_in['W3'], 'L1_gnn_b3': _L1_gnn_in['b3'], 'L1_gnn_g3': _L1_gnn_in['g3'], 'L1_gnn_beta3': _L1_gnn_in['beta3'], 'L1_gnn_W4': _L1_gnn_in['W4'], 'L1_gnn_b4': _L1_gnn_in['b4']}

def reference(x, src, dst, L0_gnn_weight1, L1_gnn_eps, L1_gnn_W1, L1_gnn_b1, L1_gnn_g1, L1_gnn_beta1, L1_gnn_W2, L1_gnn_b2, L1_gnn_g2, L1_gnn_beta2, L1_gnn_W3, L1_gnn_b3, L1_gnn_g3, L1_gnn_beta3, L1_gnn_W4, L1_gnn_b4):
    import jax
    import jax.numpy as jnp

    def _L0_gnn_ref(feat, weight1, src, dst):
        import jax, jax.numpy as jnp
        import numpy as np
        N_NODES = 3125
        agg = jax.ops.segment_sum(feat[src], dst, num_segments=N_NODES)
        h = (agg + feat) @ weight1
        h = jax.nn.relu(h)
        return h

    def _L1_gnn_ref(x, edge_index, eps, W1, b1, g1, beta1, W2, b2, g2, beta2, W3, b3, g3, beta3, W4, b4):
        import jax, jax.numpy as jnp
        import numpy as np
        BN_EPS = 1e-05
        CHANNELS = [256, 512, 1024, 512, 256]

        def _bn(h, gamma, beta):
            m = h.mean(axis=0)
            v = h.var(axis=0)
            return gamma * (h - m) * jax.lax.rsqrt(v + BN_EPS) + beta
        src, dst = (edge_index[0], edge_index[1])
        agg = jax.ops.segment_sum(x[src], dst, num_segments=x.shape[0])
        h = (1.0 + eps) * x + agg
        h = jax.nn.elu(_bn(h @ W1 + b1, g1, beta1))
        h = jax.nn.elu(_bn(h @ W2 + b2, g2, beta2))
        h = jax.nn.elu(_bn(h @ W3 + b3, g3, beta3))
        return h @ W4 + b4
    edge_index = jnp.stack([src, dst])
    h = jnp.maximum(_layernorm(x, axis=-1), 0.0)
    x = x + _L0_gnn_ref(h, L0_gnn_weight1, src, dst)
    h = jnp.maximum(_layernorm(x, axis=-1), 0.0)
    x = x + _L1_gnn_ref(h, edge_index, L1_gnn_eps, L1_gnn_W1, L1_gnn_b1, L1_gnn_g1, L1_gnn_beta1, L1_gnn_W2, L1_gnn_b2, L1_gnn_g2, L1_gnn_beta2, L1_gnn_W3, L1_gnn_b3, L1_gnn_g3, L1_gnn_beta3, L1_gnn_W4, L1_gnn_b4)
    return x

_drawn_inputs = setup_inputs


def setup_inputs(seed=0):
    import zlib

    import numpy as np

    out = dict(_drawn_inputs(seed))
    spreads = {'L1_gnn_b1': (0.0, 0.8),
     'L1_gnn_g1': (1.0, 0.2),
     'L1_gnn_beta1': (0.0, 0.8),
     'L1_gnn_b2': (0.0, 0.8),
     'L1_gnn_g2': (1.0, 0.2),
     'L1_gnn_beta2': (0.0, 0.8),
     'L1_gnn_b3': (0.0, 0.8),
     'L1_gnn_g3': (1.0, 0.2),
     'L1_gnn_beta3': (0.0, 0.447),
     'L1_gnn_b4': (0.0, 0.378)}
    factors = {}
    for name, (base, spread) in spreads.items():
        noise = np.random.default_rng([zlib.crc32(name.encode()), seed]).standard_normal(out[name].shape)
        drawn = base * np.exp(spread * noise) if base else spread * noise
        out[name] = jnp.asarray(drawn.astype(out[name].dtype))
    for name, factor in factors.items():
        out[name] = (out[name] * factor).astype(out[name].dtype)
    return out
```

```python
import concourse.bass as bass
from concourse import mybir
from contextlib import ExitStack


def gnn_two_layer_program(nc, x, src, dst, W0, eps, W1, b1, g1, be1, W2, b2, g2, be2, W3, b3, g3, be3, W4, b4, out):
    f32, f16, i32 = mybir.dt.float32, mybir.dt.float16, mybir.dt.int32
    ALU, ACT, AX = mybir.AluOpType, mybir.ActivationFunctionType, mybir.AxisListType

    N, D = x.shape
    E = src.shape[0]
    P = 128
    FULL = N // P
    REST = N - FULL * P
    NT = FULL + 1
    CW = 512
    QT = CW // P
    NC = FULL // QT
    TW = 64
    EP = 98
    ET = 4
    ROW = ET * P
    TILES = EP * ET
    EFULL = E // ROW
    ELEFT = E - EFULL * ROW
    WIN = 16
    KEYS = NT * WIN
    AW = 3168
    AW32 = AW // 2
    EDGE_HI = N - 20
    RING = 8
    NWIN = (NC * CW + TW) // WIN
    UNSPLIT = 2.0 ** -11
    SPLIT = 2.0 ** 11
    LN_EPS = BN_EPS = 1e-5
    FAR = 1.0e6
    H1, H2, H3 = W1.shape[1], W2.shape[1], W3.shape[1]
    DK, K1, K2, K3 = D // P, H1 // P, H2 // P, H3 // P
    STATS = NC + 2

    ctx = ExitStack()
    with ctx:
        def sb(stack, name, shape, dt):
            return stack.enter_context(nc.sbuf_tensor(name, shape, dt))

        def sem(name):
            return ctx.enter_context(nc.semaphore(name))

        ident = sb(ctx, "ident", [P, P], f32)
        ident16 = sb(ctx, "ident16", [P, P], f16)
        zero16 = sb(ctx, "zero16", [P, P], f16)
        self_hi = sb(ctx, "self_hi", [P, P], f16)
        self_lo = sb(ctx, "self_lo", [P, P], f16)
        epsc = sb(ctx, "epsc", [P, 6], f32)
        w0 = sb(ctx, "w0", [P, DK, D], f32)
        b4row = sb(ctx, "b4row", [P, D], f32)
        bias = {1: sb(ctx, "bias1", [P, K1], f32), 2: sb(ctx, "bias2", [P, K2], f32), 3: sb(ctx, "bias3", [P, K3], f32)}
        gamma = {1: sb(ctx, "gamma1", [P, K1], f32), 2: sb(ctx, "gamma2", [P, K2], f32), 3: sb(ctx, "gamma3", [P, K3], f32)}
        beta = {1: sb(ctx, "beta1t", [P, K1], f32), 2: sb(ctx, "beta2t", [P, K2], f32), 3: sb(ctx, "beta3t", [P, K3], f32)}
        stats = sb(ctx, "stats", [P, K2, STATS, 6], f32)
        bn_mv = sb(ctx, "bn_mv", [P, K2, 2], f32)
        bn_tmp = sb(ctx, "bn_tmp", [P, 4, K2], f32)
        bn_scale = sb(ctx, "bn_scale", [P, K2], f32)
        bn_shift = sb(ctx, "bn_shift", [P, K2], f32)
        ln_st = sb(ctx, "ln_st", [P, NT, 6], f32)
        ln_mv = sb(ctx, "ln_mv", [P, NT, 2], f32)
        ln_tmp = sb(ctx, "ln_tmp", [P, 4, NT], f32)
        lohi = sb(ctx, "lohi", [EP, 2, ET], f32)
        flag_f = sb(ctx, "flag_f", [1, 1], f32)
        flag_i = sb(ctx, "flag_i", [1, 1], i32)

        graph = ExitStack()
        counts = sb(graph, "counts", [P, NT, AW], f16)
        feat = sb(graph, "feat", [P, NT, 2 * D], f16)
        build = ExitStack()
        iota_key = sb(build, "iota_key", [P, KEYS], f16)
        iota_b = sb(build, "iota_b", [P, P], f16)
        iota_a = sb(build, "iota_a", [P, NT], f16)
        oh_key = sb(build, "oh_key", [P, RING, KEYS], f16)
        oh_b = sb(build, "oh_b", [P, RING, P], f16)
        oh_carry = sb(build, "oh_carry", [P, RING, NT], f16)
        t_key = sb(build, "t_key", [P, TILES], f32)
        t_b = sb(build, "t_b", [P, TILES], f32)
        t_carry = sb(build, "t_carry", [P, TILES], f32)
        t_a16 = sb(build, "t_a16", [P, TILES], f32)
        t_dst = sb(build, "t_dst", [P, TILES], f32)
        base_i = sb(build, "base_i", [1, TILES], i32)
        build.close()
        conv = ExitStack()
        xt = sb(conv, "xt", [P, QT, D], f32)
        hp = sb(conv, "hp", [P, QT, D], f32)
        hl = sb(conv, "hl", [P, QT, 2 * D], f16)
        u = sb(conv, "u", [P, DK, CW], f32)
        w1 = sb(conv, "w1", [P, DK, H1], f32)
        conv.close()
        graph.close()

        dense = ExitStack()
        sb(dense, "activations_in_counts", [P, 2 * K2, AW32], f32)
        w2 = sb(dense, "w2", [P, K1, H2], f32)
        w3 = sb(dense, "w3", [P, K2, H3], f32)
        w4 = sb(dense, "w4", [P, K3, D], f32)
        act_in = sb(dense, "act_in", [P, K2, CW], f32)
        e_buf = sb(dense, "e_buf", [P, 2, CW], f32)
        r_buf = sb(dense, "r_buf", [P, 2, CW], f32)
        t_buf = sb(dense, "t_buf", [P, 2, CW], f32)
        x1t = sb(dense, "x1t", [P, 2, QT, D], f32)
        ot = sb(dense, "ot", [P, 2, QT, D], f32)
        dense.close()

        ps = [ctx.enter_context(nc.psum_tensor(f"ps{i}", [P, CW], f32)) for i in range(8)]

        base_dram = nc.dram_tensor("base_dram", (2, TILES), f32, kind="Internal").ap()
        feat_dram = nc.dram_tensor("feat_dram", (NT * P, 2 * D), f16, kind="Internal").ap()
        x1_dram = nc.dram_tensor("x1_dram", (NT * P, D), f32, kind="Internal").ap()
        tiled = {n: a.rearrange("(t p) d -> p t d", p=P) for n, a in
                 (("feat", feat_dram), ("x1", x1_dram), ("x", x[0:FULL * P, :]), ("out", out[0:FULL * P, :]))}

        c32 = counts[:, :, :].bitcast(f32)
        ci32 = counts[:, :, :].bitcast(i32)
        XC = 1280
        xs = c32[:, :, XC:XC + D]
        O = WIN

        def edges(row):
            return c32[0:EP, row, O:O + ROW]

        def edges_i(row):
            return ci32[0:EP, row, O:O + ROW]

        SRC, DST, AI, BI, AF, BF, DF = range(7)
        base_b = c32[:, 14, O:O + TILES + 1]
        high_r = c32[0:1, 13, O:O + TILES]
        rel_t = c32[:, 15, O:O + TILES]
        nx_t = c32[:, 16, O:O + TILES]
        bad = c32[0:1, 8:13, O:O + TILES]

        def z(k, c, w=CW):
            if w == CW:
                return c32[:, 2 * k:2 * k + 2, bass.ds(c * (CW // 2), CW // 2)]
            return c32[:, 2 * k:2 * k + 2, NC * CW // 2:NC * CW // 2 + TW // 2]

        def two(ap, w):
            return ap.rearrange("p (a b) -> p a b", a=2)

        pads_set, edges_in, pool_ready = sem("pads_set"), sem("edges_in"), sem("pool_ready")
        x_in = [sem(f"x_in{g}") for g in range(5)]
        consts_in, eps_in = sem("consts_in"), sem("eps_in")
        dve_step, act_step, pool_step = sem("dve_step"), sem("act_step"), sem("pool_step")
        nat_ready, lohi_ready, lohi_out, rows_in = sem("nat_ready"), sem("lohi_ready"), sem("lohi_out"), sem("rows_in")
        transposed, tables_ready = sem("transposed"), sem("tables_ready")
        ln_var, ln_sd, ln_norm, ln_relu, feat_ready = sem("ln_var"), sem("ln_sd"), sem("ln_norm"), sem("ln_relu"), sem("feat_ready")
        self_ready = sem("self_ready")
        onehots, tile_used, counts_done, window_out = sem("onehots"), sem("tile_used"), sem("counts_done"), sem("window_out")
        g_step, g_onehots, g_used, g_window = sem("g_step"), sem("g_onehots"), sem("g_used"), sem("g_window")
        built = sem("built")
        agg = {l: sem(f"agg{l}") for l in (0, 1)}
        u_out = {l: sem(f"u_out{l}") for l in (0, 1)}
        lin = {l: sem(f"lin{l}") for l in (0, 1)}
        x1_done, x_tile_in, l0_step, var0, sd0, norm0 = (sem(n) for n in ("x1_done", "x_tile_in", "l0_step", "var0", "sd0", "norm0"))
        relu0, hi0, lo0, x1b_done, x1_out, feat_out = (sem(n) for n in ("relu0", "hi0", "lo0", "x1b_done", "x1_out", "feat_out"))
        tail_clear = sem("tail_clear")
        feat_in = [sem(f"feat_in{g}") for g in range(5)]
        w1_in, w_in = sem("w1_in"), {l: sem(f"w{l}_in") for l in (2, 3, 4)}
        z_out = {l: sem(f"z_out{l}") for l in (1, 2, 3)}
        stat_done = {l: sem(f"stat_done{l}") for l in (1, 2, 3)}
        bn_var = {l: sem(f"bn_var{l}") for l in (1, 2, 3)}
        bn_sd = {l: sem(f"bn_sd{l}") for l in (1, 2, 3)}
        bn_ready = {l: sem(f"bn_ready{l}") for l in (1, 2, 3)}
        er = {l: sem(f"er{l}") for l in (2, 3, 4)}
        er_used = {l: sem(f"er_used{l}") for l in (2, 3, 4)}
        act_ready = {l: sem(f"act_ready{l}") for l in (2, 3, 4)}
        act_used = {l: sem(f"act_used{l}") for l in (2, 3, 4)}
        prod = {l: sem(f"prod{l}") for l in (2, 3, 4)}
        x1_in = [sem("x1_in0"), sem("x1_in1")]
        o_done, o_sent = sem("o_done"), [sem("o_sent0"), sem("o_sent1")]

        waits_apart = sem("waits_apart")

        def wait_apart(eng, semaphore, value):
            eng.wait_ge(semaphore, value)
            eng.sem_inc(waits_apart, 1)

        POOL_SETUP = 10
        KIN = {2: K1, 3: K2, 4: K3}
        MOUT = {2: K2, 3: K3, 4: QT}
        weights = {2: w2, 3: w3, 4: w4}
        xgroups = [(0, 6), (6, 12), (12, 18), (18, 24), (24, 25)]
        block = ctx.enter_context(nc.Block())

        @block.sync
        def _(sp):
            sp.wait_ge(pads_set, 2)
            for row, arr in ((SRC, src), (DST, dst)):
                sp.dma_start(edges_i(row)[0:96, :], arr[0:96 * ROW].rearrange("(p e) -> p e", e=ROW)).then_inc(edges_in, 16)
                sp.dma_start(edges_i(row)[96:EFULL, :], arr[96 * ROW:EFULL * ROW].rearrange("(p e) -> p e", e=ROW)).then_inc(edges_in, 16)
                sp.dma_start(edges_i(row)[EFULL:EP, 0:ELEFT], arr[EFULL * ROW:E].rearrange("(p e) -> p e", p=1)).then_inc(edges_in, 16)
            sp.wait_ge(lohi_ready, 2)
            for n in range(2):
                sp.dma_start(base_dram[n, :].rearrange("(p j) -> p j", j=ET), lohi[:, n, :]).then_inc(lohi_out, 16)
            sp.wait_ge(lohi_out, 32)
            sp.wait_ge(pool_ready, POOL_SETUP)
            sp.dma_start(base_b[:, 0:TILES], base_dram[0, :].partition_broadcast(P)).then_inc(rows_in, 16)
            sp.dma_start(high_r, base_dram[1:2, :]).then_inc(rows_in, 16)

            sp.sem_inc(x1_out, 16)
            sp.sem_inc(feat_out, 16)
            sp.wait_ge(built, 2)
            sp.dma_start(w1[:, :, :], W1.rearrange("(k p) n -> p k n", p=P)).then_inc(w1_in, 16)

            def load_x(c):
                sp.wait_ge(x1_out, 16 * c + 16)
                sp.dma_start(xt[:, :, :], tiled["x"][:, bass.ds(c * QT, QT), :]).then_inc(x_tile_in, 16)

            def store(c):
                sp.wait_ge(x1b_done, c + 1)
                sp.dma_start(tiled["x1"][:, bass.ds(c * QT, QT), :], xt[:, :, :]).then_inc(x1_out, 16)
                sp.wait_ge(lo0, c + 1)
                sp.dma_start(tiled["feat"][:, bass.ds(c * QT, QT), :], hl[:, :, :]).then_inc(feat_out, 16)

            with sp.Fori(0, NC) as c:
                load_x(c)
                store(c)
            sp.wait_ge(tail_clear, 1)
            sp.dma_start(xt[0:REST, 0, :], x[FULL * P:N, :]).then_inc(x_tile_in, 16)
            sp.wait_ge(x1b_done, NC + 1)
            sp.dma_start(x1_dram[FULL * P:FULL * P + TW, :], xt[0:TW, 0, :]).then_inc(x1_out, 16)
            sp.wait_ge(lo0, NC + 1)
            sp.dma_start(feat_dram[FULL * P:FULL * P + TW, :], hl[0:TW, 0, :]).then_inc(feat_out, 16)

            sp.wait_ge(feat_out, 16 * (NC + 2))
            sp.wait_ge(agg[0], 2 * (NC + 1))
            for g, (a, b) in enumerate(xgroups[:4]):
                sp.dma_start(feat[:, a:b, :], tiled["feat"][:, a:b, :]).then_inc(feat_in[g], 16)
            sp.dma_start(feat[0:TW, FULL, :], feat_dram[FULL * P:FULL * P + TW, :]).then_inc(feat_in[4], 16)

            sp.wait_ge(agg[1], 2 * (NC + 1))
            for l, w, dram in ((2, w2, W2), (3, w3, W3), (4, w4, W4)):
                sp.dma_start(w[:, :, :], dram.rearrange("(k p) n -> p k n", p=P)).then_inc(w_in[l], 16)

            sp.wait_ge(x1_out, 16 * (NC + 2))
            sp.sem_inc(o_sent[0], 16)
            sp.sem_inc(o_sent[1], 16)

            def x1_load(c, b, lead):
                sp.dma_start(x1t[:, b, :, :], tiled["x1"][:, bass.ds(c * QT, QT), :]).then_inc(x1_in[b], 16)

            sp.wait_ge(bn_ready[1], 1)
            x1_load(0, 0, 0)
            x1_load(1, 1, 0)
            with sp.Fori(0, NC // 2 - 1) as j:
                for b in range(2):
                    c = 2 * j + b
                    sp.wait_ge(o_done, QT * (c + 3))
                    sp.dma_start(tiled["out"][:, bass.ds(c * QT, QT), :], ot[:, b, :, :]).then_inc(o_sent[b], 16)
                    x1_load(c + 2, b, 0)
            for b in range(2):
                c = NC - 2 + b
                sp.wait_ge(o_done, QT * (c + 3))
                sp.dma_start(tiled["out"][:, c * QT:(c + 1) * QT, :], ot[:, b, :, :]).then_inc(o_sent[b], 16)
                if b == 0:
                    sp.dma_start(x1t[0:TW, 0, 0, :], x1_dram[FULL * P:FULL * P + TW, :]).then_inc(x1_in[0], 16)
            sp.wait_ge(o_done, QT * (NC + 2) + 1)
            sp.dma_start(out[FULL * P:N, :], ot[0:REST, 0, 0, :]).then_inc(o_sent[0], 16)
            sp.wait_ge(o_sent[0], 16 * (NC // 2 + 2))
            sp.wait_ge(o_sent[1], 16 * (NC // 2 + 1))

        @block.gpsimd
        def _(pool):
            pool.memset(edges_i(SRC), P * NT).then_inc(pads_set, 1)
            pool.memset(edges_i(DST), N - 1).then_inc(pads_set, 1)
            pool.memset(xs[:, FULL, :], 0.0).then_inc(pool_ready, 1)
            pool.memset(ident[:, :], 0.0).then_inc(pool_ready, 1)
            pool.memset(zero16[:, :], 0.0).then_inc(pool_ready, 1)
            pool.iota(iota_key[:, :], [[1, KEYS]], base=0, channel_multiplier=0, allow_small_or_imprecise_dtypes=True).then_inc(pool_ready, 1)
            pool.iota(iota_b[:, :], [[1, P]], base=0, channel_multiplier=0, allow_small_or_imprecise_dtypes=True).then_inc(pool_ready, 1)
            pool.iota(iota_a[:, :], [[WIN, NT]], base=0, channel_multiplier=0, allow_small_or_imprecise_dtypes=True).then_inc(pool_ready, 1)
            pool.wait_ge(pool_ready, 6)
            pool.affine_select(out=ident[:, :], in_=ident[:, :], compare_op=ALU.not_equal, fill=1.0,
                               base=0, pattern=[[-1, P]], channel_multiplier=1).then_inc(pool_ready, 1)
            pool.wait_ge(pool_ready, 7)
            pool.tensor_copy(ident16[:, :], ident[:, :]).then_inc(pool_ready, 1)
            pool.memset(counts[:, :, 0:WIN], 0.0).then_inc(pool_ready, 1)
            pool.memset(counts[:, :, EDGE_HI:AW], 0.0).then_inc(pool_ready, 1)

            pool.wait_ge(consts_in, 16 * 10)

            def add_b4(c, q, p):
                pool.wait_ge(relu0, c + 1)
                pool.tensor_tensor(xt[0:p, 0:q, :], xt[0:p, 0:q, :], b4row[0:p, :].unsqueeze(1).to_broadcast([p, q, D]),
                                   ALU.add).then_inc(x1b_done, 1)

            with pool.Fori(0, NC) as c:
                add_b4(c, QT, P)
            add_b4(NC, 1, TW)

        @block.scalar
        def _(act):
            for g, (a, b) in enumerate(xgroups[:4]):
                act.dma_start(xs[:, a:b, :], tiled["x"][:, a:b, :]).then_inc(x_in[g], 16)
            act.wait_ge(pool_ready, 1)
            act.dma_start(xs[0:REST, FULL, :], x[FULL * P:N, :]).then_inc(x_in[4], 16)
            act.dma_start(w0[:, :, :], W0.rearrange("(k p) n -> p k n", p=P)).then_inc(consts_in, 16)
            with nc.allow_non_contiguous_dma(reason="channel vectors, one value per partition"):
                for l, (b_, g_, be_) in {1: (b1, g1, be1), 2: (b2, g2, be2), 3: (b3, g3, be3)}.items():
                    for t, a in ((bias[l], b_), (gamma[l], g_), (beta[l], be_)):
                        act.dma_start(t[:, :], a.rearrange("(k p) -> p k", p=P)).then_inc(consts_in, 16)
                act.dma_start(b4row[:, :], b4.partition_broadcast(P)).then_inc(eps_in, 16)
                act.dma_start(epsc[:, 0:1], eps.partition_broadcast(P)).then_inc(eps_in, 16)

            act.wait_ge(ln_var, 1)
            act.activation(ln_tmp[:, 1, :], ln_tmp[:, 0, :], ACT.Sqrt).then_inc(ln_sd, 1)
            act.wait_ge(ln_norm, 1)
            n = 0
            for g in range(5):
                for s in range(5 * g, 5 * g + 5):
                    n += 1
                    act.activation(xs[:, s, :], xs[:, s, :], ACT.Relu, bias=ln_tmp[:, 3, s:s + 1], scale=ln_tmp[:, 2, s:s + 1]).then_inc(act_step, 1)
                act.wait_ge(act_step, n)
                act.activation(feat[:, 5 * g:5 * g + 5, 0:D], xs[:, 5 * g:5 * g + 5, :], ACT.Copy).then_inc(ln_relu, 1)

            act.sem_inc(window_out, 4)
            act.sem_inc(g_window, 1)
            act.wait_ge(tables_ready, 1)
            slow = act.value_load(flag_i[0:1, 0:1])
            with act.If(slow > 0):
                with act.Fori(0, NWIN) as w:
                    wait_apart(act, g_used, (w + 1) * TILES + RING)
                    act.activation(counts[:, :, bass.ds(w * WIN, WIN)], ps[0][:, 0:KEYS].rearrange("p (a w) -> p a w", w=WIN),
                                   ACT.Copy).then_inc(g_window, 1)
            with act.Else():
                with act.Fori(0, TILES // RING) as i:
                    for t in range(RING):
                        first = act.value_load(base_i[0:1, bass.ds(i * RING + t, 1)], min_val=0, max_val=N - 1)
                        wait_apart(act, counts_done, i * RING + t + 1)
                        act.wait_ge(window_out, i * RING + t + 4)
                        act.activation(counts[:, :, bass.ds(first, WIN)], ps[t % 4][:, 0:KEYS].rearrange("p (a w) -> p a w", w=WIN),
                                       ACT.Copy).then_inc(window_out, 1)

            def sd_relu(c, q, p):
                act.wait_ge(var0, c + 1)
                act.activation(ln_tmp[0:p, 1, 0:q], ln_tmp[0:p, 0, 0:q], ACT.Sqrt).then_inc(sd0, 1)
                act.wait_ge(norm0, c + 1)
                for t in range(q):
                    ins = act.activation(hp[0:p, t, :], xt[0:p, t, :], ACT.Relu, bias=ln_tmp[0:p, 3, t:t + 1], scale=ln_tmp[0:p, 2, t:t + 1])
                ins.then_inc(relu0, 1)
                act.wait_ge(feat_out, 16 * c + 16)
                act.wait_ge(relu0, c + 1)
                act.activation(hl[0:p, 0:q, 0:D], hp[0:p, 0:q, :], ACT.Copy).then_inc(hi0, 1)

            with act.Fori(0, NC) as c:
                sd_relu(c, QT, P)
            sd_relu(NC, 1, TW)

            act.wait_ge(consts_in, 16 * 10)
            act.sem_inc(z_out[1], K1)

            def z1_out(c, w):
                for m in range(K1):
                    wait_apart(act, lin[1], K1 * c + m + 1 + K1)
                    act.activation(z(m, c, w), two(ps[m][:, 0:w], w), ACT.Identity, bias=bias[1][:, m:m + 1]).then_inc(z_out[1], 1)

            with act.Fori(0, NC) as c:
                z1_out(c, CW)
            z1_out(NC, TW)

            def bn_root(l, m):
                act.wait_ge(bn_var[l], 1)
                act.activation(bn_tmp[:, 1, 0:m], bn_tmp[:, 0, 0:m], ACT.Sqrt).then_inc(bn_sd[l], 1)
                act.wait_ge(bn_ready[l], 1)

            def exp_relu(l, c, w):
                for k in range(KIN[l]):
                    wait_apart(act, er_used[l], KIN[l] * c + k + 1)
                    act.activation(two(e_buf[:, k % 2, 0:w], w), z(k, c, w), ACT.Exp, bias=bn_shift[:, k:k + 1], scale=bn_scale[:, k:k + 1])
                    act.activation(two(r_buf[:, k % 2, 0:w], w), z(k, c, w), ACT.Relu, bias=bn_shift[:, k:k + 1], scale=bn_scale[:, k:k + 1]).then_inc(er[l], 1)

            def z_store(l, c, w, ms, bank):
                for m in ms:
                    if m == MOUT[l] - 1:
                        wait_apart(act, act_used[l], KIN[l] * (c + 2))
                    else:
                        wait_apart(act, prod[l], (MOUT[l] - 1) * c + m + 1)
                    act.activation(z(m, c, w), two(ps[bank + m][:, 0:w], w), ACT.Identity, bias=bias[l][:, m:m + 1]).then_inc(z_out[l], 1)

            HALF = K2 // 2
            bn_root(1, K1)
            act.sem_inc(z_out[2], 8)
            exp_relu(2, 0, CW)
            with act.Fori(0, NC - 1) as c:
                z_store(2, c, CW, range(HALF), 0)
                exp_relu(2, c + 1, CW)
                z_store(2, c, CW, range(HALF, K2), 0)
            z_store(2, NC - 1, CW, range(HALF), 0)
            exp_relu(2, NC, TW)
            z_store(2, NC - 1, CW, range(HALF, K2), 0)
            z_store(2, NC, TW, range(K2), 0)

            bn_root(2, K2)
            act.sem_inc(z_out[3], 8)
            exp_relu(3, 0, CW)
            with act.Fori(0, NC // 2 - 1) as j:
                for b in range(2):
                    exp_relu(3, 2 * j + b + 1, CW)
                    z_store(3, 2 * j + b, CW, range(K3), 4 * b)
            exp_relu(3, NC - 1, CW)
            z_store(3, NC - 2, CW, range(K3), 0)
            exp_relu(3, NC, TW)
            z_store(3, NC - 1, CW, range(K3), 4)
            z_store(3, NC, TW, range(K3), 0)

            bn_root(3, K3)
            with act.Fori(0, NC) as c:
                exp_relu(4, c, CW)
            exp_relu(4, NC, TW)

        @block.vector
        def _(dve):
            steps = [0]

            def done(ins):
                steps[0] += 1
                ins.then_inc(dve_step, 1)
                dve.wait_ge(dve_step, steps[0])

            def mark(ins):
                steps[0] += 1
                ins.then_inc(dve_step, 1)

            def sync():
                dve.wait_ge(dve_step, steps[0])

            dve.wait_ge(edges_in, 16 * 6)
            mark(dve.tensor_scalar(edges_i(AI), edges_i(SRC), 7, None, ALU.arith_shift_right))
            mark(dve.tensor_scalar(edges_i(BI), edges_i(SRC), P - 1, None, ALU.bitwise_and))
            mark(dve.tensor_copy(edges(DF), edges_i(DST)))
            sync()
            dve.tensor_scalar(edges(AF), edges_i(AI), float(WIN), None, ALU.mult).then_inc(nat_ready, 1)
            dve.tensor_copy(edges(BF), edges_i(BI)).then_inc(nat_ready, 1)
            by_tile = edges(DF).rearrange("p (j e) -> p j e", e=P)
            dve.tensor_reduce(lohi[:, 0, :], by_tile, AX.X, ALU.min).then_inc(lohi_ready, 1)
            dve.tensor_reduce(lohi[:, 1, :], by_tile, AX.X, ALU.max).then_inc(lohi_ready, 1)

            for g, (a, b) in enumerate(xgroups):
                dve.wait_ge(x_in[g], 16)
                for s in range(a, b):
                    mark(dve.bn_stats(ln_st[:, s, :], xs[:, s, :]))
            sync()
            for s in range(NT):
                mark(dve.bn_aggr(ln_mv[:, s, :], ln_st[:, s, :]))
            sync()
            dve.tensor_scalar(ln_tmp[:, 0, :], ln_mv[:, :, 1], LN_EPS, None, ALU.add).then_inc(ln_var, 1)
            dve.wait_ge(transposed, 3)
            for bank, t in ((0, t_a16), (1, t_b), (2, t_dst)):
                mark(dve.tensor_copy(t[:, :].rearrange("q (p j) -> q j p", j=ET), ps[bank][:, 0:TILES].rearrange("q (j p) -> q j p", j=ET)))
            dve.wait_ge(ln_sd, 1)
            done(dve.reciprocal(ln_tmp[:, 2, :], ln_tmp[:, 1, :]))
            done(dve.tensor_scalar(ln_tmp[:, 2, :], ln_tmp[:, 2, :], SPLIT, None, ALU.mult))
            dve.scalar_tensor_tensor(ln_tmp[:, 3, :], ln_mv[:, :, 0], -1.0, ln_tmp[:, 2, :], op0=ALU.mult, op1=ALU.mult).then_inc(ln_norm, 1)

            dve.wait_ge(rows_in, 32)
            mark(dve.memset(base_b[:, TILES:TILES + 1], FAR))
            mark(dve.tensor_copy(base_i[:, :], base_b[0:1, 0:TILES]))
            mark(dve.tensor_tensor(rel_t, t_dst[:, :], base_b[:, 0:TILES], ALU.subtract))
            mark(dve.memset(bad, 0.0))
            sync()
            mark(dve.tensor_tensor(nx_t, t_dst[:, :], base_b[:, 1:TILES + 1], ALU.is_equal))
            mark(dve.tensor_tensor(t_key[:, :], t_a16[:, :], rel_t, ALU.add))
            sync()
            nxt, here = base_b[0:1, 1:TILES + 1], base_b[0:1, 0:TILES]
            mark(dve.scalar_tensor_tensor(t_carry[:, :], t_a16[:, :], float(WIN), nx_t, op0=ALU.add, op1=ALU.mult))
            mark(dve.tensor_tensor(bad[:, 0, :], high_r, nxt, ALU.is_gt))
            mark(dve.tensor_tensor(bad[:, 1, :], high_r, here, ALU.subtract))
            mark(dve.tensor_tensor(bad[:, 2, 0:TILES - 1], nxt[:, 0:TILES - 1], here[:, 0:TILES - 1], ALU.subtract))
            mark(dve.tensor_scalar(bad[:, 4, 0:1], here[:, 0:1], float(WIN), None, ALU.is_gt))
            mark(dve.tensor_scalar(bad[:, 4, 1:2], here[:, TILES - 1:TILES], float(EDGE_HI - WIN), None, ALU.is_lt))
            sync()
            mark(dve.tensor_scalar(t_carry[:, :], t_carry[:, :], float(-WIN), None, ALU.add))
            mark(dve.tensor_scalar(bad[:, 1, :], bad[:, 1, :], float(WIN), None, ALU.is_ge))
            mark(dve.tensor_scalar(bad[:, 3, 0:TILES - 1], bad[:, 2, 0:TILES - 1], float(WIN), None, ALU.is_gt))
            sync()
            done(dve.tensor_scalar(bad[:, 2, 0:TILES - 1], bad[:, 2, 0:TILES - 1], 1.0, None, ALU.is_lt))
            done(dve.tensor_reduce(flag_f[:, :], bad, AX.XY, ALU.add))
            done(dve.tensor_copy(flag_i[:, :], flag_f[:, :]))
            dve.memset(flag_f[:, :], 0.0).then_inc(tables_ready, 1)

            for g in range(5):
                dve.wait_ge(ln_relu, g + 1)
                dve.tensor_tensor(feat[:, 5 * g:5 * g + 5, D:2 * D], xs[:, 5 * g:5 * g + 5, :], feat[:, 5 * g:5 * g + 5, 0:D],
                                  ALU.subtract).then_inc(feat_ready, 1)

            dve.wait_ge(eps_in, 32)
            done(dve.tensor_scalar(epsc[:, 1:2], epsc[:, 0:1], 1.0, None, ALU.add))
            done(dve.tensor_scalar(self_hi[:, :], ident16[:, :], epsc[:, 1:2], None, ALU.mult))
            done(dve.scalar_tensor_tensor(self_lo[:, :], ident16[:, :], epsc[:, 1:2], self_hi[:, :], op0=ALU.mult, op1=ALU.subtract))
            dve.memset(epsc[:, 2:3], 0.0).then_inc(self_ready, 1)

            slow = dve.value_load(flag_i[0:1, 0:1])

            def one_hots(i, half, before, used, ready, carry):
                t0 = 4 * half
                dve.wait_ge(used, before + i * RING + t0 + 4)
                dve.tensor_tensor(oh_b[:, t0:t0 + 4, :], iota_b[:, :].unsqueeze(1).to_broadcast([P, 4, P]),
                                  t_b[:, bass.ds(i * RING + t0, 4)].unsqueeze(2).to_broadcast([P, 4, P]), ALU.is_equal)
                if carry:
                    dve.tensor_tensor(oh_carry[:, t0:t0 + 4, :], iota_a[:, :].unsqueeze(1).to_broadcast([P, 4, NT]),
                                      t_carry[:, bass.ds(i * RING + t0, 4)].unsqueeze(2).to_broadcast([P, 4, NT]), ALU.is_equal)
                for t in range(t0, t0 + 4):
                    dve.tensor_scalar(oh_key[:, t, :], iota_key[:, :], t_key[:, bass.ds(i * RING + t, 1)], None, ALU.is_equal).then_inc(ready, 1)

            with dve.If(slow > 0):
                GS = 6
                with dve.Fori(0, NWIN) as w:
                    dve.wait_ge(g_used, w * TILES + RING)
                    dve.tensor_scalar(t_carry[:, :], t_dst[:, :], 0.0, None, ALU.is_ge).then_inc(g_step, 1)
                    dve.tensor_tensor(t_key[:, :], t_a16[:, :], t_dst[:, :], ALU.add).then_inc(g_step, 1)
                    dve.wait_ge(g_step, w * GS + 2)
                    dve.scalar_tensor_tensor(t_carry[:, :], t_dst[:, :], float(WIN), t_carry[:, :], op0=ALU.is_lt, op1=ALU.mult).then_inc(g_step, 1)
                    dve.wait_ge(g_step, w * GS + 3)
                    dve.scalar_tensor_tensor(t_key[:, :], t_key[:, :], 1.0, t_carry[:, :], op0=ALU.add, op1=ALU.mult).then_inc(g_step, 1)
                    dve.wait_ge(g_step, w * GS + 4)
                    dve.tensor_scalar(t_key[:, :], t_key[:, :], -1.0, None, ALU.add).then_inc(g_step, 1)
                    dve.tensor_scalar(t_dst[:, :], t_dst[:, :], float(-WIN), None, ALU.add).then_inc(g_step, 1)
                    wait_apart(dve, g_step, w * GS + 6)
                    with dve.Fori(0, TILES // RING) as i:
                        for half in range(2):
                            one_hots(i, half, w * TILES, g_used, g_onehots, False)
            with dve.Else():
                with dve.Fori(0, TILES // RING) as i:
                    for half in range(2):
                        one_hots(i, half, 0, tile_used, onehots, True)

            dve.sem_inc(u_out[0], 2)
            dve.sem_inc(u_out[1], 2)
            dve.sem_inc(x1_done, QT)
            dve.sem_inc(stat_done[1], K1)

            def u_half(l, f, c, w):
                dve.wait_ge(lin[l], (QT if l == 0 else K1) * (c + 1))
                dve.wait_ge(agg[l], 2 * c + f + 1)
                dve.tensor_scalar(u[:, f, 0:w], ps[6 + f][:, 0:w], UNSPLIT, None, ALU.mult).then_inc(u_out[l], 1)

            dve.wait_ge(built, 1)
            S0 = 4

            def x1_norm(c, q, p):
                dve.wait_ge(x_tile_in, 16 * c + 16)
                for t in range(q):
                    dve.wait_ge(lin[0], QT * c + t + 1 + QT)
                    dve.scalar_tensor_tensor(xt[0:p, t, :], ps[t][0:p, 0:D], 0.0, xt[0:p, t, :], op0=ALU.max, op1=ALU.add).then_inc(x1_done, 1)
                dve.wait_ge(x1_done, QT * c + q + QT)
                for t in range(q):
                    ins = dve.bn_stats(ln_st[0:p, t, :], xt[0:p, t, :])
                ins.then_inc(l0_step, 1)
                wait_apart(dve, l0_step, S0 * c + 1)
                for t in range(q):
                    ins = dve.bn_aggr(ln_mv[0:p, t, :], ln_st[0:p, t, :])
                ins.then_inc(l0_step, 1)
                dve.wait_ge(l0_step, S0 * c + 2)
                dve.tensor_scalar(ln_tmp[0:p, 0, 0:q], ln_mv[0:p, 0:q, 1], LN_EPS, None, ALU.add).then_inc(var0, 1)
                dve.wait_ge(sd0, c + 1)
                dve.reciprocal(ln_tmp[0:p, 2, 0:q], ln_tmp[0:p, 1, 0:q]).then_inc(l0_step, 1)
                dve.wait_ge(l0_step, S0 * c + 3)
                dve.tensor_scalar(ln_tmp[0:p, 2, 0:q], ln_tmp[0:p, 2, 0:q], SPLIT, None, ALU.mult).then_inc(l0_step, 1)
                dve.wait_ge(l0_step, S0 * c + 4)
                dve.scalar_tensor_tensor(ln_tmp[0:p, 3, 0:q], ln_mv[0:p, 0:q, 0], -1.0, ln_tmp[0:p, 2, 0:q], op0=ALU.mult, op1=ALU.mult).then_inc(norm0, 1)
                dve.wait_ge(hi0, c + 1)
                dve.tensor_tensor(hl[0:p, 0:q, D:2 * D], hp[0:p, 0:q, :], hl[0:p, 0:q, 0:D], ALU.subtract).then_inc(lo0, 1)

            u_half(0, 0, 0, CW)
            u_half(0, 1, 0, CW)
            with dve.Fori(1, NC) as c:
                u_half(0, 0, c, CW)
                x1_norm(c - 1, QT, P)
                u_half(0, 1, c, CW)
            u_half(0, 0, NC, TW)
            x1_norm(NC - 1, QT, P)
            dve.wait_ge(x1_out, 16 * (NC + 1))
            dve.memset(xt[0:TW, 0, :], 0.0).then_inc(tail_clear, 1)
            u_half(0, 1, NC, TW)
            x1_norm(NC, 1, TW)

            def z_stats(l, c, w, ms, credit):
                for m in ms:
                    dve.wait_ge(z_out[l], credit + len_m[l] * c + m + 1)
                    if w == CW:
                        dve.bn_stats(stats[:, m, bass.ds(c, 1), :], z(m, c, w)).then_inc(stat_done[l], 1)
                    else:
                        tail = z(m, c, w)
                        dve.bn_stats(stats[:, m, NC, :], tail[:, 0, 0:TW // 2])
                        dve.bn_stats(stats[:, m, NC + 1, :], tail[:, 1, 0:REST - TW // 2]).then_inc(stat_done[l], 1)

            len_m = {1: K1, 2: K2, 3: K3}

            def bn_finish(l, m, credit):
                dve.wait_ge(stat_done[l], credit + m * (NC + 1))
                for t in range(m):
                    mark(dve.bn_aggr(bn_mv[:, t, :], stats[:, t, :, :].rearrange("p c s -> p (c s)")))
                sync()
                dve.tensor_scalar(bn_tmp[:, 0, 0:m], bn_mv[:, 0:m, 1], BN_EPS, None, ALU.add).then_inc(bn_var[l], 1)
                dve.wait_ge(bn_sd[l], 1)
                done(dve.reciprocal(bn_tmp[:, 2, 0:m], bn_tmp[:, 1, 0:m]))
                done(dve.tensor_tensor(bn_scale[:, 0:m], bn_tmp[:, 2, 0:m], gamma[l][:, 0:m], ALU.mult))
                done(dve.tensor_tensor(bn_tmp[:, 3, 0:m], bn_mv[:, 0:m, 0], bn_scale[:, 0:m], ALU.mult))
                dve.tensor_tensor(bn_shift[:, 0:m], beta[l][:, 0:m], bn_tmp[:, 3, 0:m], ALU.subtract).then_inc(bn_ready[l], 1)

            u_half(1, 0, 0, CW)
            u_half(1, 1, 0, CW)
            with dve.Fori(1, NC) as c:
                u_half(1, 0, c, CW)
                z_stats(1, c - 1, CW, range(K1), K1)
                u_half(1, 1, c, CW)
            u_half(1, 0, NC, TW)
            z_stats(1, NC - 1, CW, range(K1), K1)
            u_half(1, 1, NC, TW)
            z_stats(1, NC, TW, range(K1), K1)
            dve.wait_ge(consts_in, 16 * 10)
            bn_finish(1, K1, K1)

            def elu(l, c, w):
                K = KIN[l]
                for k in range(K):
                    dve.wait_ge(er[l], K * c + k + 1)
                    dve.scalar_tensor_tensor(t_buf[:, k % 2, 0:w], e_buf[:, k % 2, 0:w], 1.0, r_buf[:, k % 2, 0:w],
                                             op0=ALU.min, op1=ALU.add).then_inc(er_used[l], 1)
                    dve.wait_ge(act_used[l], K * c + k + 1)
                    dve.wait_ge(er_used[l], K * c + k + 1 + 2)
                    dve.tensor_scalar(act_in[:, k, 0:w], t_buf[:, k % 2, 0:w], -1.0, None, ALU.add).then_inc(act_ready[l], 1)

            for l in (2, 3, 4):
                dve.sem_inc(er_used[l], 2)
            dve.sem_inc(o_done, 2 * QT)
            HALF = K2 // 2
            elu(2, 0, CW)
            with dve.Fori(0, NC - 1) as c:
                z_stats(2, c, CW, range(HALF), 8)
                elu(2, c + 1, CW)
                z_stats(2, c, CW, range(HALF, K2), 8)
            z_stats(2, NC - 1, CW, range(HALF), 8)
            elu(2, NC, TW)
            z_stats(2, NC - 1, CW, range(HALF, K2), 8)
            z_stats(2, NC, TW, range(K2), 8)
            bn_finish(2, K2, 0)

            elu(3, 0, CW)
            with dve.Fori(0, NC - 1) as c:
                elu(3, c + 1, CW)
                z_stats(3, c, CW, range(K3), 8)
            elu(3, NC, TW)
            z_stats(3, NC - 1, CW, range(K3), 8)
            z_stats(3, NC, TW, range(K3), 8)
            bn_finish(3, K3, 0)

            def add_x1(c, b, n, p, q):
                dve.wait_ge(x1_in[b], 16 * n + 16)
                dve.wait_ge(o_sent[b], 16 * n + 16)
                for t in range(q):
                    if t == QT - 1:
                        dve.wait_ge(act_used[4], K3 * (c + 2))
                    elif q == 1:
                        dve.wait_ge(act_used[4], K3 * (c + 2))
                    else:
                        dve.wait_ge(prod[4], (QT - 1) * c + t + 1)
                    dve.tensor_tensor(ot[0:p, b, t, :], ps[4 * b + t][0:p, 0:D], x1t[0:p, b, t, :], ALU.add).then_inc(o_done, 1)

            elu(4, 0, CW)
            with dve.Fori(0, NC // 2 - 1) as j:
                for b in range(2):
                    elu(4, 2 * j + b + 1, CW)
                    add_x1(2 * j + b, b, j, P, QT)
            elu(4, NC - 1, CW)
            add_x1(NC - 2, 0, NC // 2 - 1, P, QT)
            elu(4, NC, TW)
            add_x1(NC - 1, 1, NC // 2 - 1, P, QT)
            add_x1(NC, 0, NC // 2, TW, 1)

        @block.tensor
        def _(pe):
            pe.wait_ge(pool_ready, POOL_SETUP)
            pe.wait_ge(nat_ready, 2)
            pe.wait_ge(lohi_ready, 2)
            for bank, row in ((0, AF), (1, BF), (2, DF)):
                for j in range(ET):
                    ins = pe.transpose(ps[bank][:, j * EP:(j + 1) * EP], edges(row)[:, j * P:(j + 1) * P], ident[0:EP, 0:EP])
                ins.then_inc(transposed, 1)

            pe.sem_inc(tile_used, RING)
            pe.sem_inc(g_used, RING)
            pe.wait_ge(tables_ready, 1)
            slow = pe.value_load(flag_i[0:1, 0:1])

            def open_bank(bank):
                pe.matmul(ps[bank][:, 0:KEYS], zero16[:, :], iota_key[:, :], start=True, stop=False, skip_group_check=True)

            with pe.If(slow > 0):
                with pe.Fori(0, NWIN) as w:
                    pe.wait_ge(g_window, w + 1)
                    open_bank(0)
                    with pe.Fori(0, TILES // RING) as i:
                        for t in range(RING):
                            pe.wait_ge(g_onehots, w * TILES + i * RING + t + 1)
                            pe.matmul(ps[0][:, 0:KEYS], oh_b[:, t, :], oh_key[:, t, :], start=False, stop=True,
                                      skip_group_check=True).then_inc(g_used, 1)
                pe.wait_ge(g_window, NWIN + 1)
            with pe.Else():
                open_bank(0)
                with pe.Fori(0, TILES // RING) as i:
                    for t in range(RING):
                        pe.wait_ge(onehots, i * RING + t + 1)
                        pe.wait_ge(window_out, i * RING + t + 2)
                        pe.matmul(ps[t % 4][:, 0:KEYS], oh_b[:, t, :], oh_key[:, t, :], start=False, stop=True,
                                  skip_group_check=True).then_inc(counts_done, 1)
                        pe.matmul(ps[(t + 1) % 4][:, 0:KEYS:WIN], oh_b[:, t, :], oh_carry[:, t, :], start=True, stop=False,
                                  skip_group_check=True).then_inc(tile_used, 1)
                pe.wait_ge(window_out, TILES + 4)

            flat = feat[:, :, :].rearrange("p t d -> p (t d)")

            def aggregate(l, f, c, w, first=False):
                acc = ps[6 + f]
                pe.wait_ge(u_out[l], 2 * c + 1 + f)
                if w == CW:
                    cols = bass.ds(c * CW, CW)
                else:
                    cols = slice(NC * CW, NC * CW + TW)
                own = [ident16] if l == 0 else [self_hi, self_lo]
                for s in range(NT):
                    if first and l == 1 and s % 6 == 0:
                        pe.wait_ge(feat_in[s // 6], 16)
                    if first and l == 0 and s % 5 == 0:
                        pe.wait_ge(feat_ready, s // 5 + 1)
                    for part in range(2):
                        pe.matmul(acc[:, 0:w], feat[:, s, part * D + f * P:part * D + f * P + P], counts[:, s, cols],
                                  start=(s == 0 and part == 0), stop=False, skip_group_check=True)
                if w == CW:
                    for q in range(QT):
                        for part in range(2):
                            for o in own:
                                ins = pe.matmul(acc[:, q * P:(q + 1) * P], flat[:, bass.ds((c * QT + q) * 2 * D + part * D + f * P, P)],
                                                o[:, :], start=False, stop=True, skip_group_check=True)
                else:
                    for part in range(2):
                        for o in own:
                            ins = pe.matmul(acc[:, 0:w], feat[:, FULL, part * D + f * P:part * D + f * P + P], o[:, 0:w],
                                            start=False, stop=True, skip_group_check=True)
                ins.then_inc(agg[l], 1)

            def linear0(c, w):
                pe.wait_ge(u_out[0], 2 * c + 4)
                for q in range(max(1, w // P)):
                    p = min(P, w)
                    pe.wait_ge(x1_done, QT * c + q + 1)
                    for k in range(DK):
                        ins = pe.matmul(ps[q][0:p, 0:D], u[:, k, q * P:q * P + p], w0[:, k, :], start=(k == 0), stop=(k == DK - 1))
                    ins.then_inc(lin[0], 1)

            def linear1(c, w):
                pe.wait_ge(u_out[1], 2 * c + 4)
                for m in range(K1):
                    pe.wait_ge(z_out[1], K1 * c + m + 1)
                    for k in range(DK):
                        ins = pe.matmul(ps[m][:, 0:w], w1[:, k, m * P:(m + 1) * P], u[:, k, 0:w], start=(k == 0), stop=(k == DK - 1))
                    ins.then_inc(lin[1], 1)

            pe.sem_inc(built, 2)
            pe.sem_inc(lin[0], QT)
            pe.sem_inc(lin[1], K1)
            pe.wait_ge(consts_in, 16 * 10)
            for l, linear in ((0, linear0), (1, linear1)):
                if l == 1:
                    pe.wait_ge(self_ready, 1)
                    pe.wait_ge(w1_in, 16)
                aggregate(l, 0, 0, CW, first=True)
                aggregate(l, 1, 0, CW)
                with pe.Fori(1, NC) as c:
                    aggregate(l, 0, c, CW)
                    linear(c - 1, CW)
                    aggregate(l, 1, c, CW)
                aggregate(l, 0, NC, TW)
                linear(NC - 1, CW)
                aggregate(l, 1, NC, TW)
                linear(NC, TW)

            def dense_chunk(l, c, w, ms, bank, last):
                K, M = KIN[l], MOUT[l]
                for k in range(K):
                    pe.wait_ge(act_ready[l], K * c + k + 1)
                    for m in ms:
                        if k == 0:
                            pe.wait_ge(z_out[l], M * c + m + 1)
                        ins = pe.matmul(ps[bank + m][:, 0:w], weights[l][:, k, m * P:(m + 1) * P], act_in[:, k, 0:w],
                                        start=(k == 0), stop=(k == K - 1))
                        if m == M - 1:
                            ins.then_inc(act_used[l], 1)
                        elif k == K - 1:
                            ins.then_inc(prod[l], 1)

            def out_chunk(c, w, b, n):
                K = K3
                q_n, p = max(1, w // P), min(P, w)
                for k in range(K):
                    pe.wait_ge(act_ready[4], K * c + k + 1)
                    for q in range(q_n):
                        if k == 0:
                            pe.wait_ge(o_done, QT * c + q + 1)
                        ins = pe.matmul(ps[4 * b + q][0:p, 0:D], act_in[:, k, q * P:q * P + p], w4[:, k, :], start=(k == 0), stop=(k == K - 1))
                        if q == q_n - 1:
                            ins.then_inc(act_used[4], 1)
                        elif k == K - 1:
                            ins.then_inc(prod[4], 1)

            for l in (2, 3, 4):
                pe.sem_inc(act_used[l], KIN[l])
            pe.wait_ge(w_in[2], 16)
            with pe.Fori(0, NC) as c:
                dense_chunk(2, c, CW, range(K2 // 2), 0, False)
                dense_chunk(2, c, CW, range(K2 // 2, K2), 0, True)
            dense_chunk(2, NC, TW, range(K2 // 2), 0, False)
            dense_chunk(2, NC, TW, range(K2 // 2, K2), 0, True)
            pe.wait_ge(w_in[3], 16)
            with pe.Fori(0, NC // 2) as j:
                for b in range(2):
                    dense_chunk(3, 2 * j + b, CW, range(K3), 4 * b, True)
            dense_chunk(3, NC, TW, range(K3), 0, True)
            pe.wait_ge(w_in[4], 16)
            with pe.Fori(0, NC // 2) as j:
                for b in range(2):
                    out_chunk(2 * j + b, CW, b, j)
            out_chunk(NC, TW, 0, NC // 2)


_INS = ['x', 'src', 'dst', 'L0_gnn_weight1', 'L1_gnn_eps', 'L1_gnn_W1', 'L1_gnn_b1', 'L1_gnn_g1', 'L1_gnn_beta1',
        'L1_gnn_W2', 'L1_gnn_b2', 'L1_gnn_g2', 'L1_gnn_beta2', 'L1_gnn_W3', 'L1_gnn_b3', 'L1_gnn_g3', 'L1_gnn_beta3',
        'L1_gnn_W4', 'L1_gnn_b4']


def kernel(**inputs):
    import numpy as _np
    import concourse.bacc as _bacc
    from concourse import mybir as _mybir
    from concourse.bass_utils import run_bass_kernel_spmd as _run

    nc = _bacc.Bacc("TRN2", target_bir_lowering=False, num_devices=1)
    arrays, args = {}, []
    for name in _INS:
        a = _np.ascontiguousarray(inputs[name])
        arrays[f"in_{name}_dram"] = a
        args.append(nc.dram_tensor(f"in_{name}_dram", a.shape, _mybir.dt.from_np(a.dtype), kind="ExternalInput").ap())
    args.append(nc.dram_tensor("out_0_dram", inputs["x"].shape, _mybir.dt.float32, kind="ExternalOutput").ap())
    gnn_two_layer_program(nc, *args)
    r = _run(nc, [arrays], core_ids=[0])
    return r.results[0]["out_0_dram"]
```

```python
import concourse.bass as bass
from concourse import mybir
from contextlib import ExitStack


def gnn_two_layer_program(nc, x, src, dst, W0, eps, W1, b1, g1, be1, W2, b2, g2, be2, W3, b3, g3, be3, W4, b4, out):
    f32, f32r, f16, i32 = mybir.dt.float32, mybir.dt.float32r, mybir.dt.float16, mybir.dt.int32
    ALU, ACT, AX = mybir.AluOpType, mybir.ActivationFunctionType, mybir.AxisListType

    N, D = x.shape
    E = src.shape[0]
    P = 128
    FULL = N // P
    REST = N - FULL * P
    NT = FULL + 1
    CW = 512
    QT = CW // P
    NC = FULL // QT
    TW = 64
    EP = 98
    ET = 4
    ROW = ET * P
    TILES = EP * ET
    EFULL = E // ROW
    ELEFT = E - EFULL * ROW
    WIN = 14
    KEYS = NT * WIN
    AW = 3168
    AW32 = AW // 2
    EDGE_HI = N - 20
    BANKS = 8
    RING = 8
    LN_STEP = NT // 5
    X_READ = 26
    HALF_T = TILES // 2
    SAVE_STEP = 24
    NWIN = (NC * CW + TW) // WIN
    SLOTS = 4
    UNSPLIT = 2.0 ** -11
    SPLIT = 2.0 ** 11
    LN_EPS = BN_EPS = 1e-5
    FAR = 1.0e6
    H1, H2, H3 = W1.shape[1], W2.shape[1], W3.shape[1]
    DK, K1, K2, K3 = D // P, H1 // P, H2 // P, H3 // P
    STATS = NC + 2

    ctx = ExitStack()
    with ctx:
        def sb(stack, name, shape, dt):
            return stack.enter_context(nc.sbuf_tensor(name, shape, dt))

        def sem(name):
            return ctx.enter_context(nc.semaphore(name))

        ident = sb(ctx, "ident", [P, P], f32)
        ident16 = sb(ctx, "ident16", [P, P], f16)
        zero16 = sb(ctx, "zero16", [P, P], f16)
        self_hi = sb(ctx, "self_hi", [P, P], f16)
        self_lo = sb(ctx, "self_lo", [P, P], f16)
        epsc = sb(ctx, "epsc", [P, 6], f32)
        w0 = sb(ctx, "w0", [P, DK, D], f32)
        b4row = sb(ctx, "b4row", [P, D], f32)
        bias = {1: sb(ctx, "bias1", [P, K1], f32), 2: sb(ctx, "bias2", [P, K2], f32), 3: sb(ctx, "bias3", [P, K3], f32)}
        gamma = {1: sb(ctx, "gamma1", [P, K1], f32), 2: sb(ctx, "gamma2", [P, K2], f32), 3: sb(ctx, "gamma3", [P, K3], f32)}
        beta = {1: sb(ctx, "beta1t", [P, K1], f32), 2: sb(ctx, "beta2t", [P, K2], f32), 3: sb(ctx, "beta3t", [P, K3], f32)}
        stats = sb(ctx, "stats", [P, K2, STATS, 6], f32)
        bn_mv = sb(ctx, "bn_mv", [P, K2, 2], f32)
        bn_tmp = sb(ctx, "bn_tmp", [P, 4, K2], f32)
        bn_scale = sb(ctx, "bn_scale", [P, K2], f32)
        bn_shift = sb(ctx, "bn_shift", [P, K2], f32)
        ln_st = sb(ctx, "ln_st", [P, NT, 6], f32)
        ln_mv = sb(ctx, "ln_mv", [P, NT, 2], f32)
        ln_tmp = sb(ctx, "ln_tmp", [P, 4, NT], f32)
        lohi = sb(ctx, "lohi", [EP, 2, ET], f32)
        flag_f = sb(ctx, "flag_f", [1, 1], f32)
        flag_i = sb(ctx, "flag_i", [1, 1], i32)

        graph = ExitStack()
        counts = sb(graph, "counts", [P, NT, AW], f16)
        feat = sb(graph, "feat", [P, NT, 2 * D], f16)
        build = ExitStack()
        iota_key = sb(build, "iota_key", [P, KEYS], f16)
        iota_b = sb(build, "iota_b", [P, P], f16)
        iota_a = sb(build, "iota_a", [P, NT], f16)
        oh_key = sb(build, "oh_key", [P, RING, KEYS], f16)
        oh_b = sb(build, "oh_b", [P, RING, P], f16)
        oh_carry = sb(build, "oh_carry", [P, RING, NT], f16)
        t_key = sb(build, "t_key", [P, TILES], f32)
        t_b = sb(build, "t_b", [P, TILES], f32)
        t_carry = sb(build, "t_carry", [P, TILES], f32)
        t_a16 = sb(build, "t_a16", [P, TILES], f32)
        t_dst = sb(build, "t_dst", [P, TILES], f32)
        base_i = sb(build, "base_i", [1, TILES + RING], i32)
        seam = sb(build, "seam", [P, NT, WIN], f16)
        diag = sb(build, "diag", [P, P], f32)
        build.close()
        conv = ExitStack()
        xt = sb(conv, "xt", [P, QT, D], f32)
        hp = sb(conv, "hp", [P, QT, D], f32)
        hl = sb(conv, "hl", [P, QT, 2 * D], f16)
        u = sb(conv, "u", [P, DK, CW], f32)
        w1 = sb(conv, "w1", [P, DK, H1], f32)
        conv.close()
        graph.close()

        dense = ExitStack()
        sb(dense, "activations_in_counts", [P, 2 * K2, AW32], f32)
        hi_w = {2: sb(dense, "w2_hi", [P, K1, H2], f32r)}
        lo_w = {2: sb(dense, "w2_lo", [P, K1, H2], f32r)}
        hi_w[3], lo_w[3] = sb(dense, "w3_hi", [P, K2, H3], f32r), sb(dense, "w3_lo", [P, K2, H3], f32r)
        w4 = sb(dense, "w4", [P, K3, D], f32)
        act_hi = sb(dense, "act_hi", [P, SLOTS, CW], f32r)
        act_lo = sb(dense, "act_lo", [P, SLOTS, CW], f32r)
        e_buf = sb(dense, "e_buf", [P, 2, CW], f32)
        r_buf = sb(dense, "r_buf", [P, 2, CW], f32)
        t_buf = sb(dense, "t_buf", [P, 2, CW], f32)
        dense.close()
        raw = ExitStack()
        sb(raw, "activations_in_counts_", [P, 2 * K2, AW32], f32)
        sb(raw, "w2_hi_", [P, K1, H2], f32)
        raw_w = {2: sb(raw, "w2_raw", [P, K1, H2], f32)}
        sb(raw, "w3_hi_", [P, K2, H3], f32)
        raw_w[3] = sb(raw, "w3_raw", [P, K2, H3], f32)
        raw.close()
        last = ExitStack()
        sb(last, "activations_in_counts__", [P, 2 * K2, AW32], f32)
        x1t = sb(last, "x1t", [P, 2, QT, D], f32)
        ot = sb(last, "ot", [P, 2, QT, D], f32)
        act_in = sb(last, "act_in", [P, K3, CW], f32)
        last.close()

        ps = [ctx.enter_context(nc.psum_tensor(f"ps{i}", [P, CW], f32)) for i in range(8)]

        base_dram = nc.dram_tensor("base_dram", (2, TILES), f32, kind="Internal").ap()
        feat_dram = nc.dram_tensor("feat_dram", (NT * P, 2 * D), f16, kind="Internal").ap()
        x1_dram = nc.dram_tensor("x1_dram", (NT * P, D), f32, kind="Internal").ap()
        tiled = {n: a.rearrange("(t p) d -> p t d", p=P) for n, a in
                 (("feat", feat_dram), ("x1", x1_dram), ("x", x[0:FULL * P, :]), ("out", out[0:FULL * P, :]))}

        c32 = counts[:, :, :].bitcast(f32)
        ci32 = counts[:, :, :].bitcast(i32)
        XC = 1280
        xs = c32[:, :, XC:XC + D]
        O = WIN

        def in_turns(ap):
            return ap.rearrange("p (j h) -> p h j", h=2)

        def in_order(ap):
            return ap.rearrange("p (h j) -> p h j", h=2)

        def edges(row):
            return c32[0:EP, row, O:O + ROW]

        def edges_i(row):
            return ci32[0:EP, row, O:O + ROW]

        SRC, DST, AI, BI, AF, BF, DF = range(7)
        base_b = c32[:, 14, O:O + TILES + 1]
        high_r = c32[0:1, 13, O:O + TILES]
        rel_t = c32[:, 15, O:O + TILES]
        nx_t = c32[:, 16, O:O + TILES]
        bad = c32[0:1, 8:13, O:O + TILES]

        def z(k, c, w=CW):
            if w == CW:
                return c32[:, 2 * k:2 * k + 2, bass.ds(c * (CW // 2), CW // 2)]
            return c32[:, 2 * k:2 * k + 2, NC * CW // 2:NC * CW // 2 + TW // 2]

        def two(ap, w):
            return ap.rearrange("p (a b) -> p a b", a=2)

        pads_set, edges_in, pool_ready = sem("pads_set"), sem("edges_in"), sem("pool_ready")
        x_in = [sem(f"x_in{g}") for g in range(5)]
        consts_in, eps_in = sem("consts_in"), sem("eps_in")
        dve_step, act_step, pool_step = sem("dve_step"), sem("act_step"), sem("pool_step")
        nat_ready, lohi_ready, lohi_out, rows_in = sem("nat_ready"), sem("lohi_ready"), sem("lohi_out"), sem("rows_in")
        transposed, tables_ready = sem("transposed"), sem("tables_ready")
        ln_stat, ln_aggr, ln_inv, ln_y, ln_hi, self_step = (sem(n) for n in ("ln_stat", "ln_aggr", "ln_inv", "ln_y", "ln_hi", "self_step"))
        ln_var, ln_sd, ln_norm, feat_ready = sem("ln_var"), sem("ln_sd"), sem("ln_norm"), sem("feat_ready")
        self_ready = sem("self_ready")
        onehots, counts_done, window_out = sem("onehots"), sem("counts_done"), sem("window_out")
        seam_ready, seam_used, seam_saved, seam_back = (sem(n) for n in ("seam_ready", "seam_used", "seam_saved", "seam_back"))
        g_step, g_onehots, g_used, g_window = sem("g_step"), sem("g_onehots"), sem("g_used"), sem("g_window")
        built = sem("built")
        agg = {l: sem(f"agg{l}") for l in (0, 1)}
        u_out = {l: sem(f"u_out{l}") for l in (0, 1)}
        lin = {l: sem(f"lin{l}") for l in (0, 1)}
        x1_done, x_tile_in, l0_step, var0, sd0, norm0 = (sem(n) for n in ("x1_done", "x_tile_in", "l0_step", "var0", "sd0", "norm0"))
        relu0, hi0, lo0, x1b_done, x1_out, feat_out = (sem(n) for n in ("relu0", "hi0", "lo0", "x1b_done", "x1_out", "feat_out"))
        tail_clear = sem("tail_clear")
        feat_in = [sem(f"feat_in{g}") for g in range(5)]
        w1_in, w3_in, w4_in, w2_in = sem("w1_in"), sem("w3_in"), sem("w4_in"), [sem(f"w2_in{k}") for k in range(K1)]
        w_hi, w_lo = {l: sem(f"w{l}_hi_ready") for l in (2, 3)}, {l: sem(f"w{l}_lo_ready") for l in (2, 3)}
        hi_ready = {l: sem(f"hi_ready{l}") for l in (2, 3)}
        z_out = {l: sem(f"z_out{l}") for l in (1, 2, 3)}
        stat_done = {l: sem(f"stat_done{l}") for l in (1, 2, 3)}
        bn_var = {l: sem(f"bn_var{l}") for l in (1, 2, 3)}
        bn_sd = {l: sem(f"bn_sd{l}") for l in (1, 2, 3)}
        bn_ready = {l: sem(f"bn_ready{l}") for l in (1, 2, 3)}
        er = {l: sem(f"er{l}") for l in (2, 3, 4)}
        er_used = {l: sem(f"er_used{l}") for l in (2, 3, 4)}
        act_ready = {l: sem(f"act_ready{l}") for l in (2, 3, 4)}
        act_used = {l: sem(f"act_used{l}") for l in (2, 3, 4)}
        prod = {l: sem(f"prod{l}") for l in (2, 3, 4)}
        x1_in = [sem("x1_in0"), sem("x1_in1")]
        o_done, o_sent = sem("o_done"), [sem("o_sent0"), sem("o_sent1")]

        waits_apart = sem("waits_apart")

        def wait_apart(eng, semaphore, value):
            eng.wait_ge(semaphore, value)
            eng.sem_inc(waits_apart, 1)

        POOL_SETUP = 10
        KIN = {2: K1, 3: K2, 4: K3}
        MOUT = {2: K2, 3: K3, 4: QT}
        xgroups = [(0, 6), (6, 12), (12, 18), (18, 24), (24, 25)]
        block = ctx.enter_context(nc.Block())

        @block.sync
        def _(sp):
            sp.wait_ge(pads_set, 2)
            for row, arr in ((SRC, src), (DST, dst)):
                sp.dma_start(edges_i(row)[0:96, :], arr[0:96 * ROW].rearrange("(p e) -> p e", e=ROW)).then_inc(edges_in, 16)
                sp.dma_start(edges_i(row)[96:EFULL, :], arr[96 * ROW:EFULL * ROW].rearrange("(p e) -> p e", e=ROW)).then_inc(edges_in, 16)
                sp.dma_start(edges_i(row)[EFULL:EP, 0:ELEFT], arr[EFULL * ROW:E].rearrange("(p e) -> p e", p=1)).then_inc(edges_in, 16)
            sp.wait_ge(lohi_ready, 2)
            for n in range(2):
                sp.dma_start(base_dram[n, :].rearrange("(p j) -> p j", j=ET), lohi[:, n, :]).then_inc(lohi_out, 16)
            sp.wait_ge(lohi_out, 32)
            sp.wait_ge(pool_ready, POOL_SETUP)
            sp.dma_start(base_b[:, 0:TILES], base_dram[0, :].partition_broadcast(P)).then_inc(rows_in, 16)
            sp.dma_start(high_r, base_dram[1:2, :]).then_inc(rows_in, 16)

            sp.sem_inc(x1_out, 16)
            sp.sem_inc(feat_out, 16)
            sp.wait_ge(built, 2)
            sp.wait_ge(self_ready, 1)
            sp.dma_start(w1[:, :, :], W1.rearrange("(k p) n -> p k n", p=P)).then_inc(w1_in, 16)

            def load_x(c):
                sp.wait_ge(x1_out, 16 * c + 16)
                sp.dma_start(xt[:, :, :], tiled["x"][:, bass.ds(c * QT, QT), :]).then_inc(x_tile_in, 16)

            def store(c):
                sp.wait_ge(x1b_done, c + 1)
                sp.dma_start(tiled["x1"][:, bass.ds(c * QT, QT), :], xt[:, :, :]).then_inc(x1_out, 16)
                sp.wait_ge(lo0, c + 1)
                sp.dma_start(tiled["feat"][:, bass.ds(c * QT, QT), :], hl[:, :, :]).then_inc(feat_out, 16)

            with sp.Fori(0, NC) as c:
                load_x(c)
                store(c)
            sp.wait_ge(tail_clear, 1)
            sp.dma_start(xt[0:REST, 0, :], x[FULL * P:N, :]).then_inc(x_tile_in, 16)

            sp.wait_ge(agg[0], 2 * (NC + 1))
            sp.wait_ge(feat_out, 16 * (NC + 1))
            for g, (a, b) in enumerate(xgroups[:4]):
                sp.dma_start(feat[:, a:b, :], tiled["feat"][:, a:b, :]).then_inc(feat_in[g], 16)
            sp.wait_ge(x1b_done, NC + 1)
            sp.dma_start(x1_dram[FULL * P:FULL * P + TW, :], xt[0:TW, 0, :]).then_inc(x1_out, 16)
            sp.wait_ge(lo0, NC + 1)
            sp.dma_start(feat_dram[FULL * P:FULL * P + TW, :], hl[0:TW, 0, :]).then_inc(feat_out, 16)
            sp.wait_ge(feat_out, 16 * (NC + 2))
            sp.dma_start(feat[0:TW, FULL, :], feat_dram[FULL * P:FULL * P + TW, :]).then_inc(feat_in[4], 16)

            sp.wait_ge(agg[1], 2 * (NC + 1))
            for k in range(K1):
                sp.dma_start(raw_w[2][:, k, :], W2[k * P:(k + 1) * P, :]).then_inc(w2_in[k], 16)
            sp.dma_start(raw_w[3][:, :, :], W3.rearrange("(k p) n -> p k n", p=P)).then_inc(w3_in, 16)
            sp.dma_start(w4[:, :, :], W4.rearrange("(k p) n -> p k n", p=P)).then_inc(w4_in, 16)

            sp.wait_ge(x1_out, 16 * (NC + 2))
            sp.sem_inc(o_sent[0], 16)
            sp.sem_inc(o_sent[1], 16)

            def x1_load(c, b, lead):
                sp.dma_start(x1t[:, b, :, :], tiled["x1"][:, bass.ds(c * QT, QT), :]).then_inc(x1_in[b], 16)

            sp.wait_ge(bn_ready[2], 1)
            x1_load(0, 0, 0)
            x1_load(1, 1, 0)
            with sp.Fori(0, NC // 2 - 1) as j:
                for b in range(2):
                    c = 2 * j + b
                    sp.wait_ge(o_done, QT * (c + 3))
                    sp.dma_start(tiled["out"][:, bass.ds(c * QT, QT), :], ot[:, b, :, :]).then_inc(o_sent[b], 16)
                    x1_load(c + 2, b, 0)
            for b in range(2):
                c = NC - 2 + b
                sp.wait_ge(o_done, QT * (c + 3))
                sp.dma_start(tiled["out"][:, c * QT:(c + 1) * QT, :], ot[:, b, :, :]).then_inc(o_sent[b], 16)
                if b == 0:
                    sp.dma_start(x1t[0:TW, 0, 0, :], x1_dram[FULL * P:FULL * P + TW, :]).then_inc(x1_in[0], 16)
            sp.wait_ge(o_done, QT * (NC + 2) + 1)
            sp.dma_start(out[FULL * P:N, :], ot[0:REST, 0, 0, :]).then_inc(o_sent[0], 16)
            sp.wait_ge(o_sent[0], 16 * (NC // 2 + 2))
            sp.wait_ge(o_sent[1], 16 * (NC // 2 + 1))

        @block.gpsimd
        def _(pool):
            pool.memset(edges_i(SRC), P * NT).then_inc(pads_set, 1)
            pool.memset(edges_i(DST), N - 1).then_inc(pads_set, 1)
            pool.memset(xs[:, FULL, :], 0.0).then_inc(pool_ready, 1)
            pool.memset(ident[:, :], 0.0).then_inc(pool_ready, 1)
            pool.memset(zero16[:, :], 0.0).then_inc(pool_ready, 1)
            pool.iota(iota_key[:, :], [[1, KEYS]], base=0, channel_multiplier=0, allow_small_or_imprecise_dtypes=True).then_inc(pool_ready, 1)
            pool.iota(iota_b[:, :], [[1, P]], base=0, channel_multiplier=0, allow_small_or_imprecise_dtypes=True).then_inc(pool_ready, 1)
            pool.iota(iota_a[:, :], [[WIN, NT]], base=0, channel_multiplier=0, allow_small_or_imprecise_dtypes=True).then_inc(pool_ready, 1)
            pool.wait_ge(pool_ready, 6)
            pool.affine_select(out=ident[:, :], in_=ident[:, :], compare_op=ALU.not_equal, fill=1.0,
                               base=0, pattern=[[-1, P]], channel_multiplier=1).then_inc(pool_ready, 1)
            pool.wait_ge(pool_ready, 7)
            pool.tensor_copy(ident16[:, :], ident[:, :]).then_inc(pool_ready, 1)
            pool.memset(counts[:, :, 0:WIN], 0.0).then_inc(pool_ready, 1)
            pool.memset(counts[:, :, EDGE_HI:AW], 0.0).then_inc(pool_ready, 1)

            pool.wait_ge(eps_in, 32)
            pool.tensor_scalar(epsc[:, 1:2], epsc[:, 0:1], 1.0, None, ALU.add).then_inc(self_step, 1)
            pool.wait_ge(self_step, 1)
            pool.tensor_scalar(diag[:, :], ident[:, :], epsc[:, 1:2], None, ALU.mult).then_inc(self_step, 1)
            pool.wait_ge(self_step, 2)
            pool.tensor_copy(self_hi[:, :], diag[:, :]).then_inc(self_step, 1)
            pool.wait_ge(self_step, 3)
            pool.tensor_tensor(self_lo[:, :], diag[:, :], self_hi[:, :], ALU.subtract).then_inc(self_ready, 1)

            pool.wait_ge(ln_norm, 1)
            for s in range(NT):
                pool.tensor_scalar(xs[:, s, :], xs[:, s, :], ln_tmp[:, 2, s:s + 1], ln_tmp[:, 3, s:s + 1], ALU.mult, ALU.add).then_inc(ln_y, 1)
            for g in range(5):
                five = slice(5 * g, 5 * g + 5)
                pool.wait_ge(ln_y, 5 * g + 5)
                pool.tensor_scalar(xs[:, five, :], xs[:, five, :], 0.0, None, ALU.max).then_inc(ln_hi, 1)
                pool.wait_ge(ln_hi, 2 * g + 1)
                pool.tensor_copy(feat[:, five, 0:D], xs[:, five, :]).then_inc(ln_hi, 1)
                pool.wait_ge(ln_hi, 2 * g + 2)
                pool.tensor_tensor(feat[:, five, D:2 * D], xs[:, five, :], feat[:, five, 0:D], ALU.subtract).then_inc(feat_ready, 1)

            pool.wait_ge(consts_in, 16 * 10)

            def add_b4(c, q, p):
                pool.wait_ge(relu0, c + 1)
                pool.tensor_tensor(xt[0:p, 0:q, :], xt[0:p, 0:q, :], b4row[0:p, :].unsqueeze(1).to_broadcast([p, q, D]),
                                   ALU.add).then_inc(x1b_done, 1)

            with pool.Fori(0, NC) as c:
                add_b4(c, QT, P)
            add_b4(NC, 1, TW)

            pool.wait_ge(w3_in, 16)
            for k in range(K2):
                pool.tensor_copy(hi_w[3][:, k, :], raw_w[3][:, k, :]).then_inc(w_hi[3], 1)
                pool.wait_ge(w_hi[3], k + 1)
                pool.tensor_tensor(lo_w[3][:, k, :], raw_w[3][:, k, :], hi_w[3][:, k, :], ALU.subtract).then_inc(w_lo[3], 1)

        @block.scalar
        def _(act):
            for g, (a, b) in enumerate(xgroups[:4]):
                act.dma_start(xs[:, a:b, :], tiled["x"][:, a:b, :]).then_inc(x_in[g], 16)
            act.wait_ge(pool_ready, 1)
            act.dma_start(xs[0:REST, FULL, :], x[FULL * P:N, :]).then_inc(x_in[4], 16)
            act.dma_start(w0[:, :, :], W0.rearrange("(k p) n -> p k n", p=P)).then_inc(consts_in, 16)
            with nc.allow_non_contiguous_dma(reason="channel vectors, one value per partition"):
                for l, (b_, g_, be_) in {1: (b1, g1, be1), 2: (b2, g2, be2), 3: (b3, g3, be3)}.items():
                    for t, a in ((bias[l], b_), (gamma[l], g_), (beta[l], be_)):
                        act.dma_start(t[:, :], a.rearrange("(k p) -> p k", p=P)).then_inc(consts_in, 16)
                act.dma_start(b4row[:, :], b4.partition_broadcast(P)).then_inc(eps_in, 16)
                act.dma_start(epsc[:, 0:1], eps.partition_broadcast(P)).then_inc(eps_in, 16)

            def ln_root():
                act.wait_ge(ln_var, 1)
                act.activation(ln_tmp[:, 1, :], ln_tmp[:, 0, :], ACT.Sqrt).then_inc(ln_sd, 1)

            act.sem_inc(window_out, BANKS)
            act.sem_inc(g_window, 1)
            act.wait_ge(tables_ready, 1)
            slow = act.value_load(flag_i[0:1, 0:1])
            with act.If(slow > 0):
                ln_root()
                with act.Fori(0, NWIN) as w:
                    wait_apart(act, g_used, (w + 1) * TILES + RING)
                    act.activation(counts[:, :, bass.ds(w * WIN, WIN)], ps[0][:, 0:KEYS].rearrange("p (a w) -> p a w", w=WIN),
                                   ACT.Copy).then_inc(g_window, 1)
            with act.Else():
                def copy_loop(start, end):
                    with act.Fori(RING * start, RING * end, RING) as i:
                        for t0 in range(0, RING, 4):
                            _, firsts = nc.values_load_multi_w_load_instructions(
                                base_i[0:1, bass.ds(i + t0, 4)], engines=(mybir.EngineType.Activation,), min_val=0, max_val=N - 1,
                                skip_runtime_bounds_check_because="a dst of the edge list")
                            for t, first in zip(range(t0, t0 + 4), firsts):
                                if t % 2 == 0:
                                    wait_apart(act, counts_done, i + t + 2 + RING)
                                act.wait_ge(window_out, i + t + BANKS - 1)
                                act.activation(counts[:, :, bass.ds(first, WIN)],
                                               ps[t % BANKS][:, 0:KEYS].rearrange("p (a w) -> p a w", w=WIN),
                                               ACT.Copy).then_inc(window_out, 1)

                copy_loop(0, LN_STEP)
                ln_root()
                copy_loop(LN_STEP, SAVE_STEP)
                first = act.value_load(base_i[0:1, 1:2], min_val=0, max_val=N - 1)
                act.wait_ge(window_out, SAVE_STEP * RING + BANKS)
                act.activation(seam[:, :, :], counts[:, :, bass.ds(first, WIN)], ACT.Copy).then_inc(seam_saved, 1)
                copy_loop(SAVE_STEP, TILES // RING)
                first = act.value_load(base_i[0:1, 1:2], min_val=0, max_val=N - 1)
                act.wait_ge(seam_saved, 1)
                act.wait_ge(window_out, TILES + BANKS)
                act.activation(counts[:, :, bass.ds(first, WIN)], seam[:, :, :], ACT.Copy).then_inc(seam_back, 1)

            def sd_relu(c, q, p):
                act.wait_ge(var0, c + 1)
                act.activation(ln_tmp[0:p, 1, 0:q], ln_tmp[0:p, 0, 0:q], ACT.Sqrt).then_inc(sd0, 1)
                act.wait_ge(norm0, c + 1)
                for t in range(q):
                    ins = act.activation(hp[0:p, t, :], xt[0:p, t, :], ACT.Relu, bias=ln_tmp[0:p, 3, t:t + 1], scale=ln_tmp[0:p, 2, t:t + 1])
                ins.then_inc(relu0, 1)
                act.wait_ge(feat_out, 16 * c + 16)
                act.wait_ge(relu0, c + 1)
                act.activation(hl[0:p, 0:q, 0:D], hp[0:p, 0:q, :], ACT.Copy).then_inc(hi0, 1)

            with act.Fori(0, NC) as c:
                sd_relu(c, QT, P)
            sd_relu(NC, 1, TW)

            act.wait_ge(consts_in, 16 * 10)
            act.sem_inc(z_out[1], K1)

            def z1_out(c, w):
                for m in range(K1):
                    wait_apart(act, lin[1], K1 * c + m + 1 + K1)
                    act.activation(z(m, c, w), two(ps[m][:, 0:w], w), ACT.Identity, bias=bias[1][:, m:m + 1]).then_inc(z_out[1], 1)

            with act.Fori(0, NC) as c:
                z1_out(c, CW)
            z1_out(NC, TW)

            def bn_root(l, m):
                act.wait_ge(bn_var[l], 1)
                act.activation(bn_tmp[:, 1, 0:m], bn_tmp[:, 0, 0:m], ACT.Sqrt).then_inc(bn_sd[l], 1)
                if l == 1:
                    for k in range(K1):
                        act.wait_ge(w2_in[k], 16)
                        act.activation(hi_w[2][:, k, :], raw_w[2][:, k, :], ACT.Copy).then_inc(w_hi[2], 1)
                act.wait_ge(bn_ready[l], 1)

            def exp_relu(l, c, w):
                for k in range(KIN[l]):
                    wait_apart(act, er_used[l], KIN[l] * c + k + 1)
                    act.activation(two(e_buf[:, k % 2, 0:w], w), z(k, c, w), ACT.Exp, bias=bn_shift[:, k:k + 1], scale=bn_scale[:, k:k + 1])
                    act.activation(two(r_buf[:, k % 2, 0:w], w), z(k, c, w), ACT.Relu, bias=bn_shift[:, k:k + 1], scale=bn_scale[:, k:k + 1]).then_inc(er[l], 1)

            def z_store(l, c, w, ms, bank):
                for m in ms:
                    if m == MOUT[l] - 1:
                        wait_apart(act, act_used[l], KIN[l] * (c + 1) + SLOTS)
                    else:
                        wait_apart(act, prod[l], (MOUT[l] - 1) * c + m + 1)
                    act.activation(z(m, c, w), two(ps[bank + m][:, 0:w], w), ACT.Identity, bias=bias[l][:, m:m + 1]).then_inc(z_out[l], 1)

            HALF = K2 // 2
            bn_root(1, K1)
            act.sem_inc(z_out[2], 8)
            exp_relu(2, 0, CW)
            with act.Fori(0, NC - 1) as c:
                z_store(2, c, CW, range(HALF), 0)
                exp_relu(2, c + 1, CW)
                z_store(2, c, CW, range(HALF, K2), 0)
            z_store(2, NC - 1, CW, range(HALF), 0)
            exp_relu(2, NC, TW)
            z_store(2, NC - 1, CW, range(HALF, K2), 0)
            z_store(2, NC, TW, range(K2), 0)

            bn_root(2, K2)
            act.sem_inc(z_out[3], 8)
            exp_relu(3, 0, CW)
            with act.Fori(0, NC // 2 - 1) as j:
                for b in range(2):
                    exp_relu(3, 2 * j + b + 1, CW)
                    z_store(3, 2 * j + b, CW, range(K3), 4 * b)
            exp_relu(3, NC - 1, CW)
            z_store(3, NC - 2, CW, range(K3), 0)
            exp_relu(3, NC, TW)
            z_store(3, NC - 1, CW, range(K3), 4)
            z_store(3, NC, TW, range(K3), 0)

            bn_root(3, K3)
            with act.Fori(0, NC) as c:
                exp_relu(4, c, CW)
            exp_relu(4, NC, TW)

        @block.vector
        def _(dve):
            steps = [0]

            def done(ins):
                steps[0] += 1
                ins.then_inc(dve_step, 1)
                dve.wait_ge(dve_step, steps[0])

            def mark(ins):
                steps[0] += 1
                ins.then_inc(dve_step, 1)

            def sync():
                dve.wait_ge(dve_step, steps[0])

            dve.wait_ge(edges_in, 16 * 6)
            mark(dve.tensor_scalar(edges_i(AI), edges_i(SRC), 7, None, ALU.arith_shift_right))
            mark(dve.tensor_scalar(edges_i(BI), edges_i(SRC), P - 1, None, ALU.bitwise_and))
            mark(dve.tensor_copy(edges(DF), edges_i(DST)))
            sync()
            dve.tensor_scalar(edges(AF), edges_i(AI), float(WIN), None, ALU.mult).then_inc(nat_ready, 1)
            dve.tensor_copy(edges(BF), edges_i(BI)).then_inc(nat_ready, 1)
            by_tile = edges(DF).rearrange("p (j e) -> p j e", e=P)
            dve.tensor_reduce(lohi[:, 0, :], by_tile, AX.X, ALU.min).then_inc(lohi_ready, 1)
            dve.tensor_reduce(lohi[:, 1, :], by_tile, AX.X, ALU.max).then_inc(lohi_ready, 1)

            dve.wait_ge(transposed, 3)
            for bank, t in ((0, t_a16), (1, t_b), (2, t_dst)):
                for j in range(ET):
                    mark(dve.tensor_copy(t[:, :].rearrange("q (p j h) -> q j h p", j=ET, h=2)[:, j, :, :],
                                         ps[bank][:, j * EP:(j + 1) * EP].rearrange("q (h p) -> q h p", h=2)))
            sync()
            dve.wait_ge(rows_in, 32)
            mark(dve.memset(base_b[:, TILES:TILES + 1], FAR))
            mark(dve.tensor_copy(in_turns(base_i[:, 0:TILES]), in_order(base_b[0:1, 0:TILES])))
            mark(dve.tensor_tensor(in_turns(rel_t), in_turns(t_dst[:, :]), in_order(base_b[:, 0:TILES]), ALU.subtract))
            mark(dve.memset(bad, 0.0))
            sync()
            mark(dve.tensor_tensor(in_turns(nx_t), in_turns(t_dst[:, :]), in_order(base_b[:, 1:TILES + 1]), ALU.is_equal))
            mark(dve.tensor_tensor(t_key[:, :], t_a16[:, :], rel_t, ALU.add))
            sync()
            nxt, here = base_b[0:1, 1:TILES + 1], base_b[0:1, 0:TILES]
            mark(dve.scalar_tensor_tensor(t_carry[:, :], t_a16[:, :], float(WIN), nx_t, op0=ALU.add, op1=ALU.mult))
            mark(dve.tensor_tensor(bad[:, 0, :], high_r, nxt, ALU.is_gt))
            mark(dve.tensor_tensor(bad[:, 1, :], high_r, here, ALU.subtract))
            mark(dve.tensor_tensor(bad[:, 2, 0:TILES - 1], nxt[:, 0:TILES - 1], here[:, 0:TILES - 1], ALU.subtract))
            mark(dve.tensor_scalar(bad[:, 4, 0:1], here[:, 0:1], float(WIN), None, ALU.is_gt))
            mark(dve.tensor_scalar(bad[:, 4, 1:2], here[:, TILES - 1:TILES], float(EDGE_HI - WIN), None, ALU.is_lt))
            x_tile = HALF_T + X_READ * RING // 2
            mark(dve.tensor_scalar(bad[:, 4, 2:3], here[:, x_tile:x_tile + 1], float(2 * XC - WIN), None, ALU.is_gt))
            sync()
            mark(dve.tensor_scalar(t_carry[:, :], t_carry[:, :], float(-WIN), None, ALU.add))
            mark(dve.tensor_scalar(bad[:, 1, :], bad[:, 1, :], float(WIN), None, ALU.is_ge))
            mark(dve.tensor_scalar(bad[:, 3, 0:TILES - 1], bad[:, 2, 0:TILES - 1], float(WIN), None, ALU.is_gt))
            sync()
            done(dve.tensor_scalar(bad[:, 2, 0:TILES - 1], bad[:, 2, 0:TILES - 1], 1.0, None, ALU.is_lt))
            done(dve.tensor_reduce(flag_f[:, :], bad, AX.XY, ALU.add))
            done(dve.tensor_copy(flag_i[:, :], flag_f[:, :]))
            dve.memset(flag_f[:, :], 0.0).then_inc(tables_ready, 1)

            for g in range(5):
                dve.wait_ge(x_in[g], 16)

            def ln_variance():
                dve.wait_ge(ln_stat, NT)
                for s in range(NT):
                    dve.bn_aggr(ln_mv[:, s, :], ln_st[:, s, :]).then_inc(ln_aggr, 1)
                dve.wait_ge(ln_aggr, NT)
                dve.tensor_scalar(ln_tmp[:, 0, :], ln_mv[:, :, 1], LN_EPS, None, ALU.add).then_inc(ln_var, 1)

            def ln_scale_shift():
                dve.wait_ge(ln_sd, 1)
                dve.reciprocal(ln_tmp[:, 2, :], ln_tmp[:, 1, :]).then_inc(ln_inv, 1)
                dve.wait_ge(ln_inv, 1)
                dve.tensor_scalar(ln_tmp[:, 2, :], ln_tmp[:, 2, :], SPLIT, None, ALU.mult).then_inc(ln_inv, 1)
                dve.wait_ge(ln_inv, 2)
                dve.scalar_tensor_tensor(ln_tmp[:, 3, :], ln_mv[:, :, 0], -1.0, ln_tmp[:, 2, :], op0=ALU.mult, op1=ALU.mult).then_inc(ln_norm, 1)

            slow = dve.value_load(flag_i[0:1, 0:1])

            def one_hots(i, half, before, used, ready, carry):
                t0 = 4 * half
                if carry:
                    dve.wait_ge(used, i * RING + t0 + 4)
                else:
                    dve.wait_ge(used, before + i * RING + t0 + 4)
                dve.tensor_tensor(oh_b[:, t0:t0 + 4, :], iota_b[:, :].unsqueeze(1).to_broadcast([P, 4, P]),
                                  t_b[:, bass.ds(i * RING + t0, 4)].unsqueeze(2).to_broadcast([P, 4, P]), ALU.is_equal)
                if carry:
                    dve.tensor_tensor(oh_carry[:, t0:t0 + 4, :], iota_a[:, :].unsqueeze(1).to_broadcast([P, 4, NT]),
                                      t_carry[:, bass.ds(i * RING + t0, 4)].unsqueeze(2).to_broadcast([P, 4, NT]), ALU.is_equal)
                for t in range(t0, t0 + 4):
                    dve.tensor_scalar(oh_key[:, t, :], iota_key[:, :], t_key[:, bass.ds(i * RING + t, 1)], None, ALU.is_equal).then_inc(ready, 1)

            with dve.If(slow > 0):
                for s in range(NT):
                    dve.bn_stats(ln_st[:, s, :], xs[:, s, :]).then_inc(ln_stat, 1)
                ln_variance()
                ln_scale_shift()
                dve.wait_ge(feat_ready, 5)
                GS = 6
                with dve.Fori(0, NWIN) as w:
                    dve.wait_ge(g_used, w * TILES + RING)
                    dve.tensor_scalar(t_carry[:, :], t_dst[:, :], 0.0, None, ALU.is_ge).then_inc(g_step, 1)
                    dve.tensor_tensor(t_key[:, :], t_a16[:, :], t_dst[:, :], ALU.add).then_inc(g_step, 1)
                    dve.wait_ge(g_step, w * GS + 2)
                    dve.scalar_tensor_tensor(t_carry[:, :], t_dst[:, :], float(WIN), t_carry[:, :], op0=ALU.is_lt, op1=ALU.mult).then_inc(g_step, 1)
                    dve.wait_ge(g_step, w * GS + 3)
                    dve.scalar_tensor_tensor(t_key[:, :], t_key[:, :], 1.0, t_carry[:, :], op0=ALU.add, op1=ALU.mult).then_inc(g_step, 1)
                    dve.wait_ge(g_step, w * GS + 4)
                    dve.tensor_scalar(t_key[:, :], t_key[:, :], -1.0, None, ALU.add).then_inc(g_step, 1)
                    dve.tensor_scalar(t_dst[:, :], t_dst[:, :], float(-WIN), None, ALU.add).then_inc(g_step, 1)
                    wait_apart(dve, g_step, w * GS + 6)
                    with dve.Fori(0, TILES // RING) as i:
                        for half in range(2):
                            one_hots(i, half, w * TILES, g_used, g_onehots, False)
            with dve.Else():
                def one_hot_loop(start, end, stats=0):
                    with dve.Fori(start, end) as i:
                        for half in range(2):
                            one_hots(i, half, 0, counts_done, onehots, True)
                        for n in range(stats):
                            s = bass.ds(stats * i + n, 1)
                            dve.bn_stats(ln_st[:, s, :], xs[:, s, :]).then_inc(ln_stat, 1)

                dve.tensor_scalar(oh_b[:, 0, :], iota_b[:, :], t_b[:, TILES - 2:TILES - 1], None, ALU.is_equal)
                dve.tensor_scalar(oh_carry[:, 0, :], iota_a[:, :], t_carry[:, TILES - 2:TILES - 1], None, ALU.is_equal).then_inc(seam_ready, 1)
                dve.wait_ge(seam_used, 1)
                one_hot_loop(0, LN_STEP, stats=NT // LN_STEP)
                ln_variance()
                one_hot_loop(LN_STEP, LN_STEP + 2)
                ln_scale_shift()
                one_hot_loop(LN_STEP + 2, X_READ)
                dve.wait_ge(feat_ready, 5)
                one_hot_loop(X_READ, TILES // RING)

            dve.sem_inc(u_out[0], 2)
            dve.sem_inc(u_out[1], 2)
            dve.sem_inc(x1_done, QT)
            dve.sem_inc(stat_done[1], K1)

            def u_half(l, f, c, w):
                dve.wait_ge(lin[l], (QT if l == 0 else K1) * (c + 1))
                dve.wait_ge(agg[l], 2 * c + f + 1)
                dve.tensor_scalar(u[:, f, 0:w], ps[6 + f][:, 0:w], UNSPLIT, None, ALU.mult).then_inc(u_out[l], 1)

            dve.wait_ge(built, 1)
            dve.wait_ge(self_ready, 1)
            S0 = 4

            def x1_norm(c, q, p):
                dve.wait_ge(x_tile_in, 16 * c + 16)
                for t in range(q):
                    dve.wait_ge(lin[0], QT * c + t + 1 + QT)
                    dve.scalar_tensor_tensor(xt[0:p, t, :], ps[t][0:p, 0:D], 0.0, xt[0:p, t, :], op0=ALU.max, op1=ALU.add).then_inc(x1_done, 1)
                dve.wait_ge(x1_done, QT * c + q + QT)
                for t in range(q):
                    ins = dve.bn_stats(ln_st[0:p, t, :], xt[0:p, t, :])
                ins.then_inc(l0_step, 1)
                wait_apart(dve, l0_step, S0 * c + 1)
                for t in range(q):
                    ins = dve.bn_aggr(ln_mv[0:p, t, :], ln_st[0:p, t, :])
                ins.then_inc(l0_step, 1)
                dve.wait_ge(l0_step, S0 * c + 2)
                dve.tensor_scalar(ln_tmp[0:p, 0, 0:q], ln_mv[0:p, 0:q, 1], LN_EPS, None, ALU.add).then_inc(var0, 1)
                dve.wait_ge(sd0, c + 1)
                dve.reciprocal(ln_tmp[0:p, 2, 0:q], ln_tmp[0:p, 1, 0:q]).then_inc(l0_step, 1)
                dve.wait_ge(l0_step, S0 * c + 3)
                dve.tensor_scalar(ln_tmp[0:p, 2, 0:q], ln_tmp[0:p, 2, 0:q], SPLIT, None, ALU.mult).then_inc(l0_step, 1)
                dve.wait_ge(l0_step, S0 * c + 4)
                dve.scalar_tensor_tensor(ln_tmp[0:p, 3, 0:q], ln_mv[0:p, 0:q, 0], -1.0, ln_tmp[0:p, 2, 0:q], op0=ALU.mult, op1=ALU.mult).then_inc(norm0, 1)
                dve.wait_ge(hi0, c + 1)
                dve.tensor_tensor(hl[0:p, 0:q, D:2 * D], hp[0:p, 0:q, :], hl[0:p, 0:q, 0:D], ALU.subtract).then_inc(lo0, 1)

            u_half(0, 0, 0, CW)
            u_half(0, 1, 0, CW)
            with dve.Fori(1, NC) as c:
                u_half(0, 0, c, CW)
                x1_norm(c - 1, QT, P)
                u_half(0, 1, c, CW)
            u_half(0, 0, NC, TW)
            x1_norm(NC - 1, QT, P)
            dve.wait_ge(x1_out, 16 * (NC + 1))
            dve.memset(xt[0:TW, 0, :], 0.0).then_inc(tail_clear, 1)
            u_half(0, 1, NC, TW)
            x1_norm(NC, 1, TW)

            def z_stats(l, c, w, ms, credit):
                for m in ms:
                    dve.wait_ge(z_out[l], credit + len_m[l] * c + m + 1)
                    if w == CW:
                        dve.bn_stats(stats[:, m, bass.ds(c, 1), :], z(m, c, w)).then_inc(stat_done[l], 1)
                    else:
                        tail = z(m, c, w)
                        dve.bn_stats(stats[:, m, NC, :], tail[:, 0, 0:TW // 2])
                        dve.bn_stats(stats[:, m, NC + 1, :], tail[:, 1, 0:REST - TW // 2]).then_inc(stat_done[l], 1)

            len_m = {1: K1, 2: K2, 3: K3}

            def bn_finish(l, m, credit):
                dve.wait_ge(stat_done[l], credit + m * (NC + 1))
                for t in range(m):
                    mark(dve.bn_aggr(bn_mv[:, t, :], stats[:, t, :, :].rearrange("p c s -> p (c s)")))
                sync()
                dve.tensor_scalar(bn_tmp[:, 0, 0:m], bn_mv[:, 0:m, 1], BN_EPS, None, ALU.add).then_inc(bn_var[l], 1)
                dve.wait_ge(bn_sd[l], 1)
                done(dve.reciprocal(bn_tmp[:, 2, 0:m], bn_tmp[:, 1, 0:m]))
                done(dve.tensor_tensor(bn_scale[:, 0:m], bn_tmp[:, 2, 0:m], gamma[l][:, 0:m], ALU.mult))
                done(dve.tensor_tensor(bn_tmp[:, 3, 0:m], bn_mv[:, 0:m, 0], bn_scale[:, 0:m], ALU.mult))
                dve.tensor_tensor(bn_shift[:, 0:m], beta[l][:, 0:m], bn_tmp[:, 3, 0:m], ALU.subtract).then_inc(bn_ready[l], 1)

            u_half(1, 0, 0, CW)
            u_half(1, 1, 0, CW)
            with dve.Fori(1, NC) as c:
                u_half(1, 0, c, CW)
                z_stats(1, c - 1, CW, range(K1), K1)
                u_half(1, 1, c, CW)
            u_half(1, 0, NC, TW)
            z_stats(1, NC - 1, CW, range(K1), K1)
            u_half(1, 1, NC, TW)
            z_stats(1, NC, TW, range(K1), K1)
            dve.wait_ge(consts_in, 16 * 10)
            bn_finish(1, K1, K1)

            def elu(l, c, w, split_weights=False):
                K = KIN[l]
                ring = K3 if l == 4 else SLOTS
                for k in range(K):
                    if split_weights:
                        dve.wait_ge(w_hi[2], k + 1)
                        dve.tensor_tensor(lo_w[2][:, k, :], raw_w[2][:, k, :], hi_w[2][:, k, :], ALU.subtract).then_inc(w_lo[2], 1)
                    dve.wait_ge(er[l], K * c + k + 1)
                    dve.scalar_tensor_tensor(t_buf[:, k % 2, 0:w], e_buf[:, k % 2, 0:w], 1.0, r_buf[:, k % 2, 0:w],
                                             op0=ALU.min, op1=ALU.add).then_inc(er_used[l], 1)
                    dve.wait_ge(act_used[l], K * c + k + 1)
                    dve.wait_ge(er_used[l], K * c + k + 1 + 2)
                    if l == 4:
                        dve.tensor_scalar(act_in[:, k, 0:w], t_buf[:, k % 2, 0:w], -1.0, None, ALU.add).then_inc(act_ready[l], 1)
                    else:
                        hi = act_hi[:, k % ring, 0:w]
                        dve.tensor_scalar(hi, t_buf[:, k % 2, 0:w], -1.0, None, ALU.add).then_inc(hi_ready[l], 1)
                        dve.wait_ge(hi_ready[l], K * c + k + 1)
                        dve.scalar_tensor_tensor(act_lo[:, k % ring, 0:w], t_buf[:, k % 2, 0:w], -1.0, hi,
                                                 op0=ALU.add, op1=ALU.subtract).then_inc(act_ready[l], 1)

            for l in (2, 3, 4):
                dve.sem_inc(er_used[l], 2)
            dve.sem_inc(o_done, 2 * QT)
            HALF = K2 // 2
            elu(2, 0, CW, split_weights=True)
            with dve.Fori(0, NC - 1) as c:
                z_stats(2, c, CW, range(HALF), 8)
                elu(2, c + 1, CW)
                z_stats(2, c, CW, range(HALF, K2), 8)
            z_stats(2, NC - 1, CW, range(HALF), 8)
            elu(2, NC, TW)
            z_stats(2, NC - 1, CW, range(HALF, K2), 8)
            z_stats(2, NC, TW, range(K2), 8)
            bn_finish(2, K2, 0)

            elu(3, 0, CW)
            with dve.Fori(0, NC - 1) as c:
                elu(3, c + 1, CW)
                z_stats(3, c, CW, range(K3), 8)
            elu(3, NC, TW)
            z_stats(3, NC - 1, CW, range(K3), 8)
            z_stats(3, NC, TW, range(K3), 8)
            bn_finish(3, K3, 0)

            def add_x1(c, b, n, p, q):
                dve.wait_ge(x1_in[b], 16 * n + 16)
                dve.wait_ge(o_sent[b], 16 * n + 16)
                for t in range(q):
                    if t == QT - 1:
                        dve.wait_ge(act_used[4], K3 * (c + 2))
                    elif q == 1:
                        dve.wait_ge(act_used[4], K3 * (c + 2))
                    else:
                        dve.wait_ge(prod[4], (QT - 1) * c + t + 1)
                    dve.tensor_tensor(ot[0:p, b, t, :], ps[4 * b + t][0:p, 0:D], x1t[0:p, b, t, :], ALU.add).then_inc(o_done, 1)

            elu(4, 0, CW)
            with dve.Fori(0, NC // 2 - 1) as j:
                for b in range(2):
                    elu(4, 2 * j + b + 1, CW)
                    add_x1(2 * j + b, b, j, P, QT)
            elu(4, NC - 1, CW)
            add_x1(NC - 2, 0, NC // 2 - 1, P, QT)
            elu(4, NC, TW)
            add_x1(NC - 1, 1, NC // 2 - 1, P, QT)
            add_x1(NC, 0, NC // 2, TW, 1)

        @block.tensor
        def _(pe):
            pe.wait_ge(pool_ready, POOL_SETUP)
            pe.wait_ge(nat_ready, 2)
            pe.wait_ge(lohi_ready, 2)
            for bank, row in ((0, AF), (1, BF), (2, DF)):
                for j in range(ET):
                    ins = pe.transpose(ps[bank][:, j * EP:(j + 1) * EP], edges(row)[:, j * P:(j + 1) * P], ident[0:EP, 0:EP])
                ins.then_inc(transposed, 1)

            pe.sem_inc(counts_done, RING)
            pe.sem_inc(g_used, RING)
            pe.wait_ge(tables_ready, 1)
            slow = pe.value_load(flag_i[0:1, 0:1])

            def open_bank(bank):
                pe.matmul(ps[bank][:, 0:KEYS], zero16[:, :], iota_key[:, :], start=True, stop=False, skip_group_check=True)

            with pe.If(slow > 0):
                with pe.Fori(0, NWIN) as w:
                    pe.wait_ge(g_window, w + 1)
                    open_bank(0)
                    with pe.Fori(0, TILES // RING) as i:
                        for t in range(RING):
                            pe.wait_ge(g_onehots, w * TILES + i * RING + t + 1)
                            pe.matmul(ps[0][:, 0:KEYS], oh_b[:, t, :], oh_key[:, t, :], start=False, stop=True,
                                      skip_group_check=True).then_inc(g_used, 1)
                pe.wait_ge(g_window, NWIN + 1)
            with pe.Else():
                open_bank(0)
                open_bank(1)
                pe.wait_ge(seam_ready, 1)
                pe.matmul(ps[1][:, 0:KEYS:WIN], oh_b[:, 0, :], oh_carry[:, 0, :], start=False, stop=True,
                          skip_group_check=True).then_inc(seam_used, 1)
                with pe.Fori(0, TILES, RING) as i:
                    for t in range(RING):
                        if t % 2 == 0:
                            pe.wait_ge(onehots, i + t + 2)
                            pe.wait_ge(window_out, i + t + 4)
                        pe.matmul(ps[t % BANKS][:, 0:KEYS], oh_b[:, t, :], oh_key[:, t, :], start=False, stop=True,
                                  skip_group_check=True)
                        ins = pe.matmul(ps[(t + 2) % BANKS][:, 0:KEYS:WIN], oh_b[:, t, :], oh_carry[:, t, :], start=True, stop=False,
                                        skip_group_check=True)
                        if t % 2 == 1:
                            ins.then_inc(counts_done, 2)
                pe.wait_ge(window_out, TILES + BANKS)
                pe.wait_ge(seam_back, 1)

            flat = feat[:, :, :].rearrange("p t d -> p (t d)")

            def aggregate(l, f, c, w, first=False):
                acc = ps[6 + f]
                pe.wait_ge(u_out[l], 2 * c + 1 + f)
                if w == CW:
                    cols = bass.ds(c * CW, CW)
                else:
                    cols = slice(NC * CW, NC * CW + TW)
                own = [ident16] if l == 0 else [self_hi, self_lo]
                for s in range(NT):
                    if first and l == 1 and s % 6 == 0:
                        pe.wait_ge(feat_in[s // 6], 16)
                    if first and l == 0 and s % 5 == 0:
                        pe.wait_ge(feat_ready, s // 5 + 1)
                    for part in range(2):
                        pe.matmul(acc[:, 0:w], feat[:, s, part * D + f * P:part * D + f * P + P], counts[:, s, cols],
                                  start=(s == 0 and part == 0), stop=False, skip_group_check=True)
                if w == CW:
                    for q in range(QT):
                        for part in range(2):
                            for o in own:
                                ins = pe.matmul(acc[:, q * P:(q + 1) * P], flat[:, bass.ds((c * QT + q) * 2 * D + part * D + f * P, P)],
                                                o[:, :], start=False, stop=True, skip_group_check=True)
                else:
                    for part in range(2):
                        for o in own:
                            ins = pe.matmul(acc[:, 0:w], feat[:, FULL, part * D + f * P:part * D + f * P + P], o[:, 0:w],
                                            start=False, stop=True, skip_group_check=True)
                ins.then_inc(agg[l], 1)

            def linear0(c, w):
                pe.wait_ge(u_out[0], 2 * c + 4)
                for q in range(max(1, w // P)):
                    p = min(P, w)
                    pe.wait_ge(x1_done, QT * c + q + 1)
                    for k in range(DK):
                        ins = pe.matmul(ps[q][0:p, 0:D], u[:, k, q * P:q * P + p], w0[:, k, :], start=(k == 0), stop=(k == DK - 1))
                    ins.then_inc(lin[0], 1)

            def linear1(c, w):
                pe.wait_ge(u_out[1], 2 * c + 4)
                for m in range(K1):
                    pe.wait_ge(z_out[1], K1 * c + m + 1)
                    for k in range(DK):
                        ins = pe.matmul(ps[m][:, 0:w], w1[:, k, m * P:(m + 1) * P], u[:, k, 0:w], start=(k == 0), stop=(k == DK - 1))
                    ins.then_inc(lin[1], 1)

            pe.sem_inc(built, 2)
            pe.sem_inc(lin[0], QT)
            pe.sem_inc(lin[1], K1)
            pe.wait_ge(consts_in, 16 * 10)
            for l, linear in ((0, linear0), (1, linear1)):
                if l == 1:
                    pe.wait_ge(self_ready, 1)
                    pe.wait_ge(w1_in, 16)
                aggregate(l, 0, 0, CW, first=True)
                aggregate(l, 1, 0, CW)
                with pe.Fori(1, NC) as c:
                    aggregate(l, 0, c, CW)
                    linear(c - 1, CW)
                    aggregate(l, 1, c, CW)
                aggregate(l, 0, NC, TW)
                linear(NC - 1, CW)
                aggregate(l, 1, NC, TW)
                linear(NC, TW)

            def dense_chunk(l, c, w, ms, bank, first=False):
                K, M = KIN[l], MOUT[l]
                for k in range(K):
                    if first:
                        pe.wait_ge(w_lo[l], k + 1)
                    pe.wait_ge(act_ready[l], K * c + k + 1)
                    for m in ms:
                        if k == 0:
                            pe.wait_ge(z_out[l], M * c + m + 1)
                        cols = slice(m * P, (m + 1) * P)
                        for n, (wt, a) in enumerate(((hi_w, act_hi), (hi_w, act_lo), (lo_w, act_hi))):
                            ins = pe.matmul(ps[bank + m][:, 0:w], wt[l][:, k, cols], a[:, k % SLOTS, 0:w],
                                            start=(k == 0 and n == 0), stop=(k == K - 1 and n == 2))
                        if m == M - 1:
                            ins.then_inc(act_used[l], 1)
                        elif k == K - 1:
                            ins.then_inc(prod[l], 1)

            def out_chunk(c, w, b, n):
                K = K3
                q_n, p = max(1, w // P), min(P, w)
                for k in range(K):
                    pe.wait_ge(act_ready[4], K * c + k + 1)
                    for q in range(q_n):
                        if k == 0:
                            pe.wait_ge(o_done, QT * c + q + 1)
                        ins = pe.matmul(ps[4 * b + q][0:p, 0:D], act_in[:, k, q * P:q * P + p], w4[:, k, :], start=(k == 0), stop=(k == K - 1))
                        if q == q_n - 1:
                            ins.then_inc(act_used[4], 1)
                        elif k == K - 1:
                            ins.then_inc(prod[4], 1)

            for l in (2, 3, 4):
                pe.sem_inc(act_used[l], SLOTS)
            low, high = range(K2 // 2), range(K2 // 2, K2)
            dense_chunk(2, 0, CW, low, 0, first=True)
            dense_chunk(2, 0, CW, high, 0)
            with pe.Fori(1, NC) as c:
                dense_chunk(2, c, CW, low, 0)
                dense_chunk(2, c, CW, high, 0)
            dense_chunk(2, NC, TW, low, 0)
            dense_chunk(2, NC, TW, high, 0)
            dense_chunk(3, 0, CW, range(K3), 0, first=True)
            with pe.Fori(0, NC // 2 - 1) as j:
                for b in range(2):
                    dense_chunk(3, 2 * j + b + 1, CW, range(K3), 4 * (1 - b))
            dense_chunk(3, NC - 1, CW, range(K3), 4)
            dense_chunk(3, NC, TW, range(K3), 0)
            pe.wait_ge(w4_in, 16)
            with pe.Fori(0, NC // 2) as j:
                for b in range(2):
                    out_chunk(2 * j + b, CW, b, j)
            out_chunk(NC, TW, 0, NC // 2)


_INS = ['x', 'src', 'dst', 'L0_gnn_weight1', 'L1_gnn_eps', 'L1_gnn_W1', 'L1_gnn_b1', 'L1_gnn_g1', 'L1_gnn_beta1',
        'L1_gnn_W2', 'L1_gnn_b2', 'L1_gnn_g2', 'L1_gnn_beta2', 'L1_gnn_W3', 'L1_gnn_b3', 'L1_gnn_g3', 'L1_gnn_beta3',
        'L1_gnn_W4', 'L1_gnn_b4']


def kernel(**inputs):
    import numpy as _np
    import concourse.bacc as _bacc
    from concourse import mybir as _mybir
    from concourse.bass_utils import run_bass_kernel_spmd as _run

    nc = _bacc.Bacc("TRN2", target_bir_lowering=False, num_devices=1)
    arrays, args = {}, []
    for name in _INS:
        a = _np.ascontiguousarray(inputs[name])
        arrays[f"in_{name}_dram"] = a
        args.append(nc.dram_tensor(f"in_{name}_dram", a.shape, _mybir.dt.from_np(a.dtype), kind="ExternalInput").ap())
    args.append(nc.dram_tensor("out_0_dram", inputs["x"].shape, _mybir.dt.float32, kind="ExternalOutput").ap())
    gnn_two_layer_program(nc, *args)
    r = _run(nc, [arrays], core_ids=[0])
    return r.results[0]["out_0_dram"]
```

```python
import concourse.bass as bass
from concourse import mybir
from contextlib import ExitStack


def gnn_two_layer_program(nc, x, src, dst, W0, eps, W1, b1, g1, be1, W2, b2, g2, be2, W3, b3, g3, be3, W4, b4, out):
    f32, f32r, f16, i32 = mybir.dt.float32, mybir.dt.float32r, mybir.dt.float16, mybir.dt.int32
    ALU, ACT, AX = mybir.AluOpType, mybir.ActivationFunctionType, mybir.AxisListType

    N, D = x.shape
    E = src.shape[0]
    P = 128
    FULL = N // P
    REST = N - FULL * P
    NT = FULL + 1
    CW = 512
    QT = CW // P
    NC = FULL // QT
    TW = -(-(N - NC * CW) // 64) * 64
    ET = 4
    ROW = ET * P
    EP = -(-E // ROW)
    TILES = EP * ET
    EFULL = E // ROW
    ELEFT = E - EFULL * ROW
    WIN = 14
    KEYS = NT * WIN
    AW = NC * CW + TW + 32
    AW32 = AW // 2
    EDGE_HI = N - 20
    BANKS = 6
    RING = 8
    LN_EARLY = 15
    LAP = 24
    LAPS = TILES // LAP
    EARLY = {0: (8, 12, 6), 1: (13, LAPS, 8)}
    EVAC_STEP = 37
    LN_STEP = 5
    X_READ = 26
    HALF_T = TILES // 2
    SAVE_STEP = 8
    NWIN = (NC * CW + TW) // WIN
    SLOTS = 4
    UNSPLIT = 2.0 ** -11
    SPLIT = 2.0 ** 11
    assert TILES % RING == 0 and TILES % 2 == 0 and (LAPS * LAP) % BANKS == 0 and LAP % RING == 0
    assert (NC * CW + TW) % WIN == 0 and NC % 2 == 0 and FULL % QT == 0
    LN_EPS = BN_EPS = 1e-5
    FAR = 1.0e6
    H1, H2, H3 = W1.shape[1], W2.shape[1], W3.shape[1]
    DK, K1, K2, K3 = D // P, H1 // P, H2 // P, H3 // P
    STATS = NC + 2

    ctx = ExitStack()
    with ctx:
        def sb(stack, name, shape, dt):
            return stack.enter_context(nc.sbuf_tensor(name, shape, dt))

        def sem(name):
            return ctx.enter_context(nc.semaphore(name))

        ident = sb(ctx, "ident", [P, P], f32)
        ident16 = sb(ctx, "ident16", [P, P], f16)
        zero16 = sb(ctx, "zero16", [P, P], f16)
        self_hi = sb(ctx, "self_hi", [P, P], f16)
        self_lo = sb(ctx, "self_lo", [P, P], f16)
        epsc = sb(ctx, "epsc", [P, 6], f32)
        w0 = sb(ctx, "w0", [P, DK, D], f32)
        b4row = sb(ctx, "b4row", [P, D], f32)
        bias = {1: sb(ctx, "bias1", [P, K1], f32), 2: sb(ctx, "bias2", [P, K2], f32), 3: sb(ctx, "bias3", [P, K3], f32)}
        gamma = {1: sb(ctx, "gamma1", [P, K1], f32), 2: sb(ctx, "gamma2", [P, K2], f32), 3: sb(ctx, "gamma3", [P, K3], f32)}
        beta = {1: sb(ctx, "beta1t", [P, K1], f32), 2: sb(ctx, "beta2t", [P, K2], f32), 3: sb(ctx, "beta3t", [P, K3], f32)}
        stats = sb(ctx, "stats", [P, K2, STATS, 6], f32)
        bn_mv = sb(ctx, "bn_mv", [P, K2, 2], f32)
        bn_tmp = sb(ctx, "bn_tmp", [P, 4, K2], f32)
        bn_scale = sb(ctx, "bn_scale", [P, K2], f32)
        bn_shift = sb(ctx, "bn_shift", [P, K2], f32)
        table = sb(ctx, "table", [P, 8], f32)
        ln_st = sb(ctx, "ln_st", [P, NT, 6], f32)
        ln_mv = sb(ctx, "ln_mv", [P, NT, 2], f32)
        ln_tmp = sb(ctx, "ln_tmp", [P, 4, NT], f32)
        lohi = sb(ctx, "lohi", [EP, 2, ET], f32)
        flag_f = sb(ctx, "flag_f", [1, 1], f32)
        flag_i = sb(ctx, "flag_i", [1, 1], i32)

        graph = ExitStack()
        counts = sb(graph, "counts", [P, NT, AW], f16)
        feat = sb(graph, "feat", [P, NT, 2 * D], f16)
        build = ExitStack()
        iota_key = sb(build, "iota_key", [P, KEYS], f16)
        iota_b = sb(build, "iota_b", [P, P], f16)
        iota_a = sb(build, "iota_a", [P, NT], f16)
        oh_key = sb(build, "oh_key", [P, RING, KEYS], f16)
        oh_b = sb(build, "oh_b", [P, RING, P], f16)
        oh_carry = sb(build, "oh_carry", [P, RING, NT], f16)
        t_key = sb(build, "t_key", [P, TILES], f32)
        t_b = sb(build, "t_b", [P, TILES], f32)
        sb(build, "pad_to_u", [P, 48], f16)
        t_a16 = sb(build, "t_a16", [P, TILES], f32)
        t_dst = sb(build, "t_dst", [P, TILES], f32)
        diag = sb(build, "diag", [P, P], f32)
        sb(build, "pad_after_u", [P, 112], f32)
        t_carry = sb(build, "t_carry", [P, TILES], f32)
        base_i = sb(build, "base_i", [1, TILES + LAP], i32)
        seam = sb(build, "seam", [P, NT, WIN], f16)
        build.close()
        conv = ExitStack()
        xt = sb(conv, "xt", [P, QT, D], f32)
        hp = sb(conv, "hp", [P, QT, D], f32)
        hl = sb(conv, "hl", [P, QT, 2 * D], f16)
        u = sb(conv, "u", [P, DK, CW], f32)
        w1 = sb(conv, "w1", [P, DK, H1], f32)
        conv.close()
        conv1 = ExitStack()
        w1_hi = sb(conv1, "w1_hi", [P, DK, H1], f32r)
        w1_lo = sb(conv1, "w1_lo", [P, DK, H1], f32r)
        u_lo = sb(conv1, "u_lo", [P, DK, CW], f32r)
        u_hi = sb(conv1, "u_hi", [P, DK, CW], f32r)
        w2_first = sb(conv1, "w2_first", [P, H2], f32)
        conv1.close()
        graph.close()

        dense = ExitStack()
        sb(dense, "activations_in_counts", [P, 2 * K2, AW32], f32)
        hi_w = {2: sb(dense, "w2_hi", [P, K1, H2], f32r)}
        lo_w = {2: sb(dense, "w2_lo", [P, K1, H2], f32r)}
        hi_w[3], lo_w[3] = sb(dense, "w3_hi", [P, K2, H3], f32r), sb(dense, "w3_lo", [P, K2, H3], f32r)
        w4 = sb(dense, "w4", [P, K3, D], f32)
        act_hi = sb(dense, "act_hi", [P, SLOTS, CW], f32r)
        act_lo = sb(dense, "act_lo", [P, SLOTS, CW], f32r)
        e_buf = sb(dense, "e_buf", [P, 2, CW], f32)
        r_buf = sb(dense, "r_buf", [P, 2, CW], f32)
        t_buf = sb(dense, "t_buf", [P, 2, CW], f32)
        dense.close()
        raw = ExitStack()
        sb(raw, "activations_in_counts_", [P, 2 * K2, AW32], f32)
        sb(raw, "w2_hi_", [P, K1, H2], f32)
        raw_w = {2: sb(raw, "w2_raw", [P, K1, H2], f32)}
        sb(raw, "w3_hi_", [P, K2, H3], f32)
        raw_w[3] = sb(raw, "w3_raw", [P, K2, H3], f32)
        raw.close()
        last = ExitStack()
        sb(last, "activations_in_counts__", [P, 2 * K2, AW32], f32)
        x1t = sb(last, "x1t", [P, 2, QT, D], f32)
        ot = sb(last, "ot", [P, 2, QT, D], f32)
        act_in = sb(last, "act_in", [P, K3, CW], f32)
        last.close()

        ps = [ctx.enter_context(nc.psum_tensor(f"ps{i}", [P, CW], f32)) for i in range(8)]

        base_dram = nc.dram_tensor("base_dram", (2, TILES), f32, kind="Internal").ap()
        feat_dram = nc.dram_tensor("feat_dram", (NT * P, 2 * D), f16, kind="Internal").ap()
        x1_dram = nc.dram_tensor("x1_dram", (NT * P, D), f32, kind="Internal").ap()
        tiled = {n: a.rearrange("(t p) d -> p t d", p=P) for n, a in
                 (("feat", feat_dram), ("x1", x1_dram), ("x", x[0:FULL * P, :]), ("out", out[0:FULL * P, :]))}

        c32 = counts[:, :, :].bitcast(f32)
        ci32 = counts[:, :, :].bitcast(i32)
        XC = NC * CW // 2 - D
        xs = c32[:, :, XC:XC + D]
        O = WIN

        def in_turns(ap):
            return ap.rearrange("p (j h) -> p h j", h=2)

        def in_order(ap):
            return ap.rearrange("p (h j) -> p h j", h=2)

        def edges(row):
            return c32[0:EP, row, O:O + ROW]

        def edges_i(row):
            return ci32[0:EP, row, O:O + ROW]

        SRC, DST, AI, BI, AF, BF, DF = range(7)
        base_b = c32[:, 14, O:O + TILES + 1]
        high_r = c32[0:1, 13, O:O + TILES]
        rel_t = c32[:, 15, O:O + TILES]
        nx_t = c32[:, 16, O:O + TILES]
        bad = c32[0:1, 8:13, O:O + TILES]

        def z(k, c, w=CW):
            if w == CW:
                return c32[:, 2 * k:2 * k + 2, bass.ds(c * (CW // 2), CW // 2)]
            return c32[:, 2 * k:2 * k + 2, NC * CW // 2:NC * CW // 2 + TW // 2]

        def two(ap, w):
            return ap.rearrange("p (a b) -> p a b", a=2)

        pads_set, edges_in, pool_ready = sem("pads_set"), sem("edges_in"), sem("pool_ready")
        x_in = [sem(f"x_in{g}") for g in range(5)]
        consts_in, eps_in = sem("consts_in"), sem("eps_in")
        dve_step = sem("dve_step")
        nat_ready, lohi_ready, lohi_out, rows_in = sem("nat_ready"), sem("lohi_ready"), sem("lohi_out"), sem("rows_in")
        transposed, tables_ready = sem("transposed"), sem("tables_ready")
        ln_stat, ln_aggr, ln_inv, ln_y, ln_hi, self_step = (sem(n) for n in ("ln_stat", "ln_aggr", "ln_inv", "ln_y", "ln_hi", "self_step"))
        ln_var, ln_sd, ln_norm, feat_ready = sem("ln_var"), sem("ln_sd"), sem("ln_norm"), sem("feat_ready")
        self_ready = sem("self_ready")
        onehots, counts_done, window_out = sem("onehots"), sem("counts_done"), sem("window_out")
        seam_ready, seam_used, seam_saved, seam_back = (sem(n) for n in ("seam_ready", "seam_used", "seam_saved", "seam_back"))
        g_step, g_onehots, g_used, g_window = sem("g_step"), sem("g_onehots"), sem("g_used"), sem("g_window")
        built = sem("built")
        agg = {l: sem(f"agg{l}") for l in (0, 1)}
        u_out = {l: sem(f"u_out{l}") for l in (0, 1)}
        lin = {l: sem(f"lin{l}") for l in (0, 1)}
        x1_done, x_tile_in, l0_step, var0, sd0, norm0 = (sem(n) for n in ("x1_done", "x_tile_in", "l0_step", "var0", "sd0", "norm0"))
        relu0, hi0, lo0, x1b_done, x1_out, feat_out = (sem(n) for n in ("relu0", "hi0", "lo0", "x1b_done", "x1_out", "feat_out"))
        tail_clear = sem("tail_clear")
        feat_in = [sem(f"feat_in{g}") for g in range(5)]
        w1_in, w3_in, w4_in, w2_in = sem("w1_in"), sem("w3_in"), sem("w4_in"), [sem(f"w2_in{k}") for k in range(K1)]
        u_hi_ready, w1_hi_ready, w1_lo_ready = sem("u_hi_ready"), sem("w1_hi_ready"), sem("w1_lo_ready")
        w_hi, w_lo = {l: sem(f"w{l}_hi_ready") for l in (2, 3)}, {l: sem(f"w{l}_lo_ready") for l in (2, 3)}
        hi_ready = {l: sem(f"hi_ready{l}") for l in (2, 3)}
        z_out = {l: sem(f"z_out{l}") for l in (1, 2, 3)}
        stat_done = {l: sem(f"stat_done{l}") for l in (1, 2, 3)}
        bn_var = {l: sem(f"bn_var{l}") for l in (1, 2, 3)}
        bn_sd = {l: sem(f"bn_sd{l}") for l in (1, 2, 3)}
        bn_ready = {l: sem(f"bn_ready{l}") for l in (1, 2, 3)}
        er = {l: sem(f"er{l}") for l in (2, 3, 4)}
        er_used = {l: sem(f"er_used{l}") for l in (2, 3, 4)}
        act_ready = {l: sem(f"act_ready{l}") for l in (2, 3, 4)}
        act_used = {l: sem(f"act_used{l}") for l in (2, 3, 4)}
        prod = {l: sem(f"prod{l}") for l in (2, 3, 4)}
        x1_in = [sem("x1_in0"), sem("x1_in1")]
        o_done, o_sent = sem("o_done"), [sem("o_sent0"), sem("o_sent1")]

        waits_apart = sem("waits_apart")

        def wait_apart(eng, semaphore, value):
            eng.wait_ge(semaphore, value)
            eng.sem_inc(waits_apart, 1)

        POOL_SETUP = 10
        KIN = {2: K1, 3: K2, 4: K3}
        MOUT = {2: K2, 3: K3, 4: QT}
        xgroups = [(0, 6), (6, 12), (12, 18), (18, 24), (24, 25)]
        block = ctx.enter_context(nc.Block())

        @block.sync
        def _(sp):
            sp.wait_ge(pads_set, 2)
            for row, arr in ((SRC, src), (DST, dst)):
                sp.dma_start(edges_i(row)[0:96, :], arr[0:96 * ROW].rearrange("(p e) -> p e", e=ROW)).then_inc(edges_in, 16)
                sp.dma_start(edges_i(row)[96:EFULL, :], arr[96 * ROW:EFULL * ROW].rearrange("(p e) -> p e", e=ROW)).then_inc(edges_in, 16)
                sp.dma_start(edges_i(row)[EFULL:EP, 0:ELEFT], arr[EFULL * ROW:E].rearrange("(p e) -> p e", p=1)).then_inc(edges_in, 16)
            sp.wait_ge(lohi_ready, 2)
            for n in range(2):
                sp.dma_start(base_dram[n, :].rearrange("(p j) -> p j", j=ET), lohi[:, n, :]).then_inc(lohi_out, 16)
            sp.wait_ge(lohi_out, 32)
            sp.wait_ge(pool_ready, POOL_SETUP)
            sp.dma_start(base_b[:, 0:TILES], base_dram[0, :].partition_broadcast(P)).then_inc(rows_in, 16)
            sp.dma_start(high_r, base_dram[1:2, :]).then_inc(rows_in, 16)

            sp.sem_inc(x1_out, 16)
            sp.sem_inc(feat_out, 16)
            sp.wait_ge(built, 2)
            sp.wait_ge(self_ready, 1)
            sp.dma_start(w1[:, :, :], W1.rearrange("(k p) n -> p k n", p=P)).then_inc(w1_in, 16)

            def load_x(c):
                sp.wait_ge(x1_out, 16 * c + 16)
                sp.dma_start(xt[:, :, :], tiled["x"][:, bass.ds(c * QT, QT), :]).then_inc(x_tile_in, 16)

            def store(c):
                sp.wait_ge(x1b_done, c + 1)
                sp.dma_start(tiled["x1"][:, bass.ds(c * QT, QT), :], xt[:, :, :]).then_inc(x1_out, 16)
                sp.wait_ge(lo0, c + 1)
                sp.dma_start(tiled["feat"][:, bass.ds(c * QT, QT), :], hl[:, :, :]).then_inc(feat_out, 16)

            with sp.Fori(0, NC - 1) as c:
                load_x(c)
                store(c)
            load_x(NC - 1)
            sp.wait_ge(agg[0], 2 * (NC + 1))
            sp.wait_ge(feat_out, 16 * NC)
            for g, (a, b) in enumerate(xgroups[:3]):
                sp.dma_start(feat[:, a:b, :], tiled["feat"][:, a:b, :]).then_inc(feat_in[g], 16)
            store(NC - 1)
            sp.wait_ge(tail_clear, 1)
            sp.dma_start(xt[0:REST, 0, :], x[FULL * P:N, :]).then_inc(x_tile_in, 16)

            sp.wait_ge(feat_out, 16 * (NC + 1))
            a, b = xgroups[3]
            sp.dma_start(feat[:, a:b, :], tiled["feat"][:, a:b, :]).then_inc(feat_in[3], 16)
            sp.wait_ge(x1b_done, NC + 1)
            sp.dma_start(x1_dram[FULL * P:FULL * P + TW, :], xt[0:TW, 0, :]).then_inc(x1_out, 16)
            sp.wait_ge(lo0, NC + 1)
            sp.dma_start(feat_dram[FULL * P:FULL * P + TW, :], hl[0:TW, 0, :]).then_inc(feat_out, 16)
            sp.wait_ge(feat_out, 16 * (NC + 2))
            sp.dma_start(feat[0:TW, FULL, :], feat_dram[FULL * P:FULL * P + TW, :]).then_inc(feat_in[4], 16)

            sp.wait_ge(w1_lo_ready, 1)
            sp.dma_start(w2_first[:, :], W2[0:P, :]).then_inc(w2_in[0], 16)

            sp.wait_ge(agg[1], 2 * (NC + 1))
            for k in range(1, K1):
                sp.dma_start(raw_w[2][:, k, :], W2[k * P:(k + 1) * P, :]).then_inc(w2_in[k], 16)
            sp.dma_start(raw_w[3][:, :, :], W3.rearrange("(k p) n -> p k n", p=P)).then_inc(w3_in, 16)
            sp.dma_start(w4[:, :, :], W4.rearrange("(k p) n -> p k n", p=P)).then_inc(w4_in, 16)

            sp.wait_ge(x1_out, 16 * (NC + 2))
            sp.sem_inc(o_sent[0], 16)
            sp.sem_inc(o_sent[1], 16)

            def x1_load(c, b):
                sp.dma_start(x1t[:, b, :, :], tiled["x1"][:, bass.ds(c * QT, QT), :]).then_inc(x1_in[b], 16)

            sp.wait_ge(bn_ready[2], 1)
            x1_load(0, 0)
            x1_load(1, 1)
            with sp.Fori(0, NC // 2 - 1) as j:
                for b in range(2):
                    c = 2 * j + b
                    sp.wait_ge(o_done, QT * (c + 3))
                    sp.dma_start(tiled["out"][:, bass.ds(c * QT, QT), :], ot[:, b, :, :]).then_inc(o_sent[b], 16)
                    x1_load(c + 2, b)
            for b in range(2):
                c = NC - 2 + b
                sp.wait_ge(o_done, QT * (c + 3))
                sp.dma_start(tiled["out"][:, c * QT:(c + 1) * QT, :], ot[:, b, :, :]).then_inc(o_sent[b], 16)
                if b == 0:
                    sp.dma_start(x1t[0:TW, 0, 0, :], x1_dram[FULL * P:FULL * P + TW, :]).then_inc(x1_in[0], 16)
            sp.wait_ge(o_done, QT * (NC + 2) + 1)
            sp.dma_start(out[FULL * P:N, :], ot[0:REST, 0, 0, :]).then_inc(o_sent[0], 16)
            sp.wait_ge(o_sent[0], 16 * (NC // 2 + 2))
            sp.wait_ge(o_sent[1], 16 * (NC // 2 + 1))

        @block.gpsimd
        def _(pool):
            pool.memset(edges_i(SRC), P * NT).then_inc(pads_set, 1)
            pool.memset(edges_i(DST), N - 1).then_inc(pads_set, 1)
            pool.memset(xs[:, FULL, :], 0.0).then_inc(pool_ready, 1)
            pool.memset(ident[:, :], 0.0).then_inc(pool_ready, 1)
            pool.memset(zero16[:, :], 0.0).then_inc(pool_ready, 1)
            pool.iota(iota_key[:, :], [[1, KEYS]], base=0, channel_multiplier=0, allow_small_or_imprecise_dtypes=True).then_inc(pool_ready, 1)
            pool.iota(iota_b[:, :], [[1, P]], base=0, channel_multiplier=0, allow_small_or_imprecise_dtypes=True).then_inc(pool_ready, 1)
            pool.iota(iota_a[:, :], [[WIN, NT]], base=0, channel_multiplier=0, allow_small_or_imprecise_dtypes=True).then_inc(pool_ready, 1)
            pool.wait_ge(pool_ready, 6)
            pool.affine_select(out=ident[:, :], in_=ident[:, :], compare_op=ALU.not_equal, fill=1.0,
                               base=0, pattern=[[-1, P]], channel_multiplier=1).then_inc(pool_ready, 1)
            pool.wait_ge(pool_ready, 7)
            pool.tensor_copy(ident16[:, :], ident[:, :]).then_inc(pool_ready, 1)
            pool.memset(counts[:, :, 0:WIN], 0.0).then_inc(pool_ready, 1)
            pool.memset(counts[:, :, EDGE_HI:AW], 0.0).then_inc(pool_ready, 1)

            pool.wait_ge(eps_in, 32)
            pool.tensor_scalar(epsc[:, 1:2], epsc[:, 0:1], 1.0, None, ALU.add).then_inc(self_step, 1)
            pool.wait_ge(self_step, 1)
            pool.tensor_scalar(diag[:, :], ident[:, :], epsc[:, 1:2], None, ALU.mult).then_inc(self_step, 1)
            pool.wait_ge(self_step, 2)
            pool.tensor_copy(self_hi[:, :], diag[:, :]).then_inc(self_step, 1)
            pool.wait_ge(self_step, 3)
            pool.tensor_tensor(self_lo[:, :], diag[:, :], self_hi[:, :], ALU.subtract).then_inc(self_ready, 1)

            pool.wait_ge(ln_norm, 1)
            for s in range(NT):
                pool.tensor_scalar(xs[:, s, :], xs[:, s, :], ln_tmp[:, 2, s:s + 1], ln_tmp[:, 3, s:s + 1], ALU.mult, ALU.add).then_inc(ln_y, 1)
            for g in range(5):
                five = slice(5 * g, 5 * g + 5)
                pool.wait_ge(ln_y, 5 * g + 5)
                pool.tensor_scalar(xs[:, five, :], xs[:, five, :], 0.0, None, ALU.max).then_inc(ln_hi, 1)
                pool.wait_ge(ln_hi, 2 * g + 1)
                pool.tensor_copy(feat[:, five, 0:D], xs[:, five, :]).then_inc(ln_hi, 1)
                pool.wait_ge(ln_hi, 2 * g + 2)
                pool.tensor_tensor(feat[:, five, D:2 * D], xs[:, five, :], feat[:, five, 0:D], ALU.subtract).then_inc(feat_ready, 1)

            pool.wait_ge(consts_in, 16 * 10)

            def add_b4(c, q, p):
                pool.wait_ge(relu0, c + 1)
                pool.tensor_tensor(xt[0:p, 0:q, :], xt[0:p, 0:q, :], b4row[0:p, :].unsqueeze(1).to_broadcast([p, q, D]),
                                   ALU.add).then_inc(x1b_done, 1)

            with pool.Fori(0, NC) as c:
                add_b4(c, QT, P)
            add_b4(NC, 1, TW)

            pool.wait_ge(w1_in, 16)
            pool.wait_ge(x1_out, 16 * (NC + 2))
            pool.wait_ge(lo0, NC + 1)
            pool.tensor_copy(w1_hi[:, :, :], w1[:, :, :]).then_inc(w1_hi_ready, 1)
            pool.wait_ge(w1_hi_ready, 1)
            pool.tensor_tensor(w1_lo[:, :, :], w1[:, :, :], w1_hi[:, :, :], ALU.subtract).then_inc(w1_lo_ready, 1)

            pool.wait_ge(w3_in, 16)
            for k in range(K2):
                pool.tensor_copy(hi_w[3][:, k, :], raw_w[3][:, k, :]).then_inc(w_hi[3], 1)
                pool.wait_ge(w_hi[3], k + 1)
                pool.tensor_tensor(lo_w[3][:, k, :], raw_w[3][:, k, :], hi_w[3][:, k, :], ALU.subtract).then_inc(w_lo[3], 1)

        @block.scalar
        def _(act):
            act.wait_ge(edges_in, 16 * 6)
            for g, (a, b) in enumerate(xgroups[:4]):
                act.dma_start(xs[:, a:b, :], tiled["x"][:, a:b, :]).then_inc(x_in[g], 16)
            act.wait_ge(pool_ready, 1)
            act.dma_start(xs[0:REST, FULL, :], x[FULL * P:N, :]).then_inc(x_in[4], 16)
            act.dma_start(w0[:, :, :], W0.rearrange("(k p) n -> p k n", p=P)).then_inc(consts_in, 16)
            with nc.allow_non_contiguous_dma(reason="channel vectors, one value per partition"):
                for l, (b_, g_, be_) in {1: (b1, g1, be1), 2: (b2, g2, be2), 3: (b3, g3, be3)}.items():
                    for t, a in ((bias[l], b_), (gamma[l], g_), (beta[l], be_)):
                        act.dma_start(t[:, :], a.rearrange("(k p) -> p k", p=P)).then_inc(consts_in, 16)
                act.dma_start(b4row[:, :], b4.partition_broadcast(P)).then_inc(eps_in, 16)
                act.dma_start(epsc[:, 0:1], eps.partition_broadcast(P)).then_inc(eps_in, 16)

            def ln_root():
                act.wait_ge(ln_var, 1)
                act.activation(ln_tmp[:, 1, :], ln_tmp[:, 0, :], ACT.Sqrt).then_inc(ln_sd, 1)

            tables = [0]

            def load_table(function):
                act.activation(table[:, tables[0]:tables[0] + 1], ident[:, 0:1], function)
                tables[0] += 1

            act.wait_ge(pool_ready, POOL_SETUP)
            load_table(ACT.Sqrt)

            act.sem_inc(window_out, BANKS)
            act.sem_inc(g_window, 1)
            act.wait_ge(tables_ready, 1)
            slow = act.value_load(flag_i[0:1, 0:1])
            with act.If(slow > 0):
                ln_root()
                with act.Fori(0, NWIN) as w:
                    wait_apart(act, g_used, (w + 1) * TILES + RING)
                    act.activation(counts[:, :, bass.ds(w * WIN, WIN)], ps[0][:, 0:KEYS].rearrange("p (a w) -> p a w", w=WIN),
                                   ACT.Copy).then_inc(g_window, 1)
            with act.Else():
                def copy_windows(i, count):
                    for t0 in range(0, count, 4):
                        _, firsts = nc.values_load_multi_w_load_instructions(
                            base_i[0:1, bass.ds(i + t0, 4)], engines=(mybir.EngineType.Activation,), min_val=0, max_val=N - 1,
                            skip_runtime_bounds_check_because="a dst of the edge list")
                        for t, first in zip(range(t0, t0 + 4), firsts):
                            if t % 2 == 0:
                                wait_apart(act, counts_done, i + t + 2 + RING)
                            act.wait_ge(window_out, i + t + BANKS - 1)
                            act.activation(counts[:, :, bass.ds(first, WIN)],
                                           ps[t % BANKS][:, 0:KEYS].rearrange("p (a w) -> p a w", w=WIN),
                                           ACT.Copy).then_inc(window_out, 1)

                def copy_loop(start, end):
                    with act.Fori(LAP * start, LAP * end, LAP) as i:
                        copy_windows(i, LAP)

                copy_loop(0, 2)
                ln_root()
                copy_loop(2, SAVE_STEP)
                first = act.value_load(base_i[0:1, 1:2], min_val=0, max_val=N - 1)
                act.wait_ge(window_out, SAVE_STEP * LAP + BANKS)
                act.activation(seam[:, :, :], counts[:, :, bass.ds(first, WIN)], ACT.Copy).then_inc(seam_saved, 1)
                copy_loop(SAVE_STEP, LAPS)
                copy_windows(LAPS * LAP, TILES - LAPS * LAP)
                first = act.value_load(base_i[0:1, 1:2], min_val=0, max_val=N - 1)
                act.wait_ge(seam_saved, 1)
                act.wait_ge(window_out, TILES + BANKS)
                act.activation(counts[:, :, bass.ds(first, WIN)], seam[:, :, :], ACT.Copy).then_inc(seam_back, 1)

            def sd_relu(c, q, p):
                act.wait_ge(var0, c + 1)
                act.activation(ln_tmp[0:p, 1, 0:q], ln_tmp[0:p, 0, 0:q], ACT.Sqrt).then_inc(sd0, 1)
                act.wait_ge(norm0, c + 1)
                for t in range(q):
                    ins = act.activation(hp[0:p, t, :], xt[0:p, t, :], ACT.Relu, bias=ln_tmp[0:p, 3, t:t + 1], scale=ln_tmp[0:p, 2, t:t + 1])
                ins.then_inc(relu0, 1)
                act.wait_ge(feat_out, 16 * c + 16)
                act.wait_ge(relu0, c + 1)
                act.activation(hl[0:p, 0:q, 0:D], hp[0:p, 0:q, :], ACT.Copy).then_inc(hi0, 1)

            with act.Fori(0, NC) as c:
                sd_relu(c, QT, P)
            sd_relu(NC, 1, TW)

            act.wait_ge(consts_in, 16 * 10)
            act.sem_inc(z_out[1], K1)

            def z1_out(c, w):
                for m in range(K1):
                    wait_apart(act, lin[1], K1 * c + m + 1 + K1)
                    act.activation(z(m, c, w), two(ps[m][:, 0:w], w), ACT.Identity, bias=bias[1][:, m:m + 1]).then_inc(z_out[1], 1)

            with act.Fori(0, NC) as c:
                z1_out(c, CW)
            z1_out(NC, TW)

            def split_w2(k):
                act.wait_ge(w2_in[k], 16)
                act.activation(hi_w[2][:, k, :], w2_first[:, :] if k == 0 else raw_w[2][:, k, :], ACT.Copy).then_inc(w_hi[2], 1)

            def bn_root(l, m):
                load_table(ACT.Sqrt)
                if l == 1:
                    split_w2(0)
                act.wait_ge(bn_var[l], 1)
                act.activation(bn_tmp[:, 1, 0:m], bn_tmp[:, 0, 0:m], ACT.Sqrt).then_inc(bn_sd[l], 1)
                load_table(ACT.Exp)
                if l == 1:
                    split_w2(1)
                act.wait_ge(bn_ready[l], 1)

            def exp_relu(l, c, w, split_weights=False):
                for k in range(KIN[l]):
                    wait_apart(act, er_used[l], KIN[l] * c + k + 1)
                    act.activation(two(e_buf[:, k % 2, 0:w], w), z(k, c, w), ACT.Exp, bias=bn_shift[:, k:k + 1], scale=bn_scale[:, k:k + 1])
                    act.activation(two(r_buf[:, k % 2, 0:w], w), z(k, c, w), ACT.Relu, bias=bn_shift[:, k:k + 1], scale=bn_scale[:, k:k + 1]).then_inc(er[l], 1)
                    if split_weights and k + 2 < K1:
                        split_w2(k + 2)

            def z_store(l, c, w, ms, bank):
                for m in ms:
                    if m == MOUT[l] - 1:
                        wait_apart(act, act_used[l], KIN[l] * (c + 1) + SLOTS)
                    else:
                        wait_apart(act, prod[l], (MOUT[l] - 1) * c + m + 1)
                    act.activation(z(m, c, w), two(ps[bank + m][:, 0:w], w), ACT.Identity, bias=bias[l][:, m:m + 1]).then_inc(z_out[l], 1)

            HALF = K2 // 2
            bn_root(1, K1)
            act.sem_inc(z_out[2], 8)
            exp_relu(2, 0, CW, split_weights=True)
            with act.Fori(0, NC - 1) as c:
                z_store(2, c, CW, range(HALF), 0)
                exp_relu(2, c + 1, CW)
                z_store(2, c, CW, range(HALF, K2), 0)
            z_store(2, NC - 1, CW, range(HALF), 0)
            exp_relu(2, NC, TW)
            z_store(2, NC - 1, CW, range(HALF, K2), 0)
            z_store(2, NC, TW, range(K2), 0)

            bn_root(2, K2)
            act.sem_inc(z_out[3], 8)
            exp_relu(3, 0, CW)
            with act.Fori(0, NC // 2 - 1) as j:
                for b in range(2):
                    exp_relu(3, 2 * j + b + 1, CW)
                    z_store(3, 2 * j + b, CW, range(K3), 4 * b)
            exp_relu(3, NC - 1, CW)
            z_store(3, NC - 2, CW, range(K3), 0)
            exp_relu(3, NC, TW)
            z_store(3, NC - 1, CW, range(K3), 4)
            z_store(3, NC, TW, range(K3), 0)

            bn_root(3, K3)
            exp_relu(4, 0, CW)
            with act.Fori(1, NC) as c:
                exp_relu(4, c, CW)
            exp_relu(4, NC, TW)

        @block.vector
        def _(dve):
            steps = [0]

            def done(ins):
                steps[0] += 1
                ins.then_inc(dve_step, 1)
                dve.wait_ge(dve_step, steps[0])

            def mark(ins):
                steps[0] += 1
                ins.then_inc(dve_step, 1)

            def sync():
                dve.wait_ge(dve_step, steps[0])

            dve.wait_ge(edges_in, 16 * 6)
            mark(dve.tensor_scalar(edges_i(AI), edges_i(SRC), 7, None, ALU.arith_shift_right))
            mark(dve.tensor_scalar(edges_i(BI), edges_i(SRC), P - 1, None, ALU.bitwise_and))
            mark(dve.tensor_copy(edges(DF), edges_i(DST)))
            sync()
            dve.tensor_scalar(edges(AF), edges_i(AI), float(WIN), None, ALU.mult).then_inc(nat_ready, 1)
            dve.tensor_copy(edges(BF), edges_i(BI)).then_inc(nat_ready, 1)
            by_tile = edges(DF).rearrange("p (j e) -> p j e", e=P)
            dve.tensor_reduce(lohi[:, 0, :], by_tile, AX.X, ALU.min).then_inc(lohi_ready, 1)
            dve.tensor_reduce(lohi[:, 1, :], by_tile, AX.X, ALU.max).then_inc(lohi_ready, 1)

            dve.wait_ge(transposed, 3)
            for bank, t in ((0, t_a16), (1, t_b), (2, t_dst)):
                for j in range(ET):
                    mark(dve.tensor_copy(t[:, :].rearrange("q (p j h) -> q j h p", j=ET, h=2)[:, j, :, :],
                                         ps[bank][:, j * EP:(j + 1) * EP].rearrange("q (h p) -> q h p", h=2)))
            for s in range(LN_EARLY):
                if s % 6 == 0:
                    dve.wait_ge(x_in[s // 6], 16)
                dve.bn_stats(ln_st[:, s, :], xs[:, s, :]).then_inc(ln_stat, 1)
            sync()
            dve.wait_ge(rows_in, 32)
            mark(dve.memset(base_b[:, TILES:TILES + 1], FAR))
            mark(dve.tensor_copy(in_turns(base_i[:, 0:TILES]), in_order(base_b[0:1, 0:TILES])))
            mark(dve.tensor_tensor(in_turns(rel_t), in_turns(t_dst[:, :]), in_order(base_b[:, 0:TILES]), ALU.subtract))
            mark(dve.memset(bad, 0.0))
            sync()
            mark(dve.tensor_tensor(in_turns(nx_t), in_turns(t_dst[:, :]), in_order(base_b[:, 1:TILES + 1]), ALU.is_equal))
            mark(dve.tensor_tensor(t_key[:, :], t_a16[:, :], rel_t, ALU.add))
            sync()
            nxt, here = base_b[0:1, 1:TILES + 1], base_b[0:1, 0:TILES]
            mark(dve.scalar_tensor_tensor(t_carry[:, :], t_a16[:, :], float(WIN), nx_t, op0=ALU.add, op1=ALU.mult))
            mark(dve.tensor_tensor(bad[:, 0, :], high_r, nxt, ALU.is_gt))
            mark(dve.tensor_tensor(bad[:, 1, :], high_r, here, ALU.subtract))
            mark(dve.tensor_tensor(bad[:, 2, 0:TILES - 1], nxt[:, 0:TILES - 1], here[:, 0:TILES - 1], ALU.subtract))
            mark(dve.tensor_scalar(bad[:, 4, 0:1], here[:, 0:1], float(WIN), None, ALU.is_gt))
            mark(dve.tensor_scalar(bad[:, 4, 1:2], here[:, TILES - 1:TILES], float(EDGE_HI - WIN), None, ALU.is_lt))
            for c, (lap, _, _) in EARLY.items():
                tile = lap * LAP // 2 - 1
                mark(dve.tensor_scalar(bad[:, 4, 3 + c:4 + c], here[:, tile:tile + 1], float((c + 1) * CW), None, ALU.is_lt))
            x_tile = HALF_T + X_READ * RING // 2
            mark(dve.tensor_scalar(bad[:, 4, 2:3], here[:, x_tile:x_tile + 1], float(2 * XC - WIN), None, ALU.is_gt))
            sync()
            mark(dve.tensor_scalar(t_carry[:, :], t_carry[:, :], float(-WIN), None, ALU.add))
            mark(dve.tensor_scalar(bad[:, 1, :], bad[:, 1, :], float(WIN), None, ALU.is_ge))
            mark(dve.tensor_scalar(bad[:, 3, 0:TILES - 1], bad[:, 2, 0:TILES - 1], float(WIN), None, ALU.is_gt))
            sync()
            done(dve.tensor_scalar(bad[:, 2, 0:TILES - 1], bad[:, 2, 0:TILES - 1], 1.0, None, ALU.is_lt))
            done(dve.tensor_reduce(flag_f[:, :], bad, AX.XY, ALU.add))
            done(dve.tensor_copy(flag_i[:, :], flag_f[:, :]))
            dve.memset(flag_f[:, :], 0.0).then_inc(tables_ready, 1)

            for g in range(5):
                dve.wait_ge(x_in[g], 16)

            def ln_variance():
                dve.wait_ge(ln_stat, NT)
                for s in range(NT):
                    dve.bn_aggr(ln_mv[:, s, :], ln_st[:, s, :]).then_inc(ln_aggr, 1)
                dve.wait_ge(ln_aggr, NT)
                dve.tensor_scalar(ln_tmp[:, 0, :], ln_mv[:, :, 1], LN_EPS, None, ALU.add).then_inc(ln_var, 1)

            def ln_scale_shift():
                dve.wait_ge(ln_sd, 1)
                dve.reciprocal(ln_tmp[:, 2, :], ln_tmp[:, 1, :]).then_inc(ln_inv, 1)
                dve.wait_ge(ln_inv, 1)
                dve.tensor_scalar(ln_tmp[:, 2, :], ln_tmp[:, 2, :], SPLIT, None, ALU.mult).then_inc(ln_inv, 1)
                dve.wait_ge(ln_inv, 2)
                dve.scalar_tensor_tensor(ln_tmp[:, 3, :], ln_mv[:, :, 0], -1.0, ln_tmp[:, 2, :], op0=ALU.mult, op1=ALU.mult).then_inc(ln_norm, 1)

            slow = dve.value_load(flag_i[0:1, 0:1])

            dve.sem_inc(u_out[0], 2)
            dve.sem_inc(u_out[1], 2)

            def u_half(l, f, c, w):
                dve.wait_ge(lin[l], (QT if l == 0 else K1) * (c + 1))
                dve.wait_ge(agg[l], 2 * c + f + 1)
                if l == 0:
                    dve.tensor_scalar(u[:, f, 0:w], ps[6 + f][:, 0:w], UNSPLIT, None, ALU.mult).then_inc(u_out[l], 1)
                else:
                    dve.tensor_scalar(u_hi[:, f, 0:w], ps[6 + f][:, 0:w], UNSPLIT, None, ALU.mult).then_inc(u_hi_ready, 1)
                    dve.wait_ge(u_hi_ready, 2 * c + f + 1)
                    dve.scalar_tensor_tensor(u_lo[:, f, 0:w], ps[6 + f][:, 0:w], UNSPLIT, u_hi[:, f, 0:w],
                                             op0=ALU.mult, op1=ALU.subtract).then_inc(u_out[l], 1)

            def one_hots(i, half, before, used, ready, carry):
                t0 = 4 * half
                dve.wait_ge(used, before + i * RING + t0 + 4)
                dve.tensor_tensor(oh_b[:, t0:t0 + 4, :], iota_b[:, :].unsqueeze(1).to_broadcast([P, 4, P]),
                                  t_b[:, bass.ds(i * RING + t0, 4)].unsqueeze(2).to_broadcast([P, 4, P]), ALU.is_equal)
                if carry:
                    dve.tensor_tensor(oh_carry[:, t0:t0 + 4, :], iota_a[:, :].unsqueeze(1).to_broadcast([P, 4, NT]),
                                      t_carry[:, bass.ds(i * RING + t0, 4)].unsqueeze(2).to_broadcast([P, 4, NT]), ALU.is_equal)
                for t in range(t0, t0 + 4):
                    dve.tensor_scalar(oh_key[:, t, :], iota_key[:, :], t_key[:, bass.ds(i * RING + t, 1)], None, ALU.is_equal).then_inc(ready, 1)

            with dve.If(slow > 0):
                for s in range(LN_EARLY, NT):
                    dve.bn_stats(ln_st[:, s, :], xs[:, s, :]).then_inc(ln_stat, 1)
                ln_variance()
                ln_scale_shift()
                dve.wait_ge(feat_ready, 5)
                GS = 6
                with dve.Fori(0, NWIN) as w:
                    dve.wait_ge(g_used, w * TILES + RING)
                    dve.tensor_scalar(t_carry[:, :], t_dst[:, :], 0.0, None, ALU.is_ge).then_inc(g_step, 1)
                    dve.tensor_tensor(t_key[:, :], t_a16[:, :], t_dst[:, :], ALU.add).then_inc(g_step, 1)
                    dve.wait_ge(g_step, w * GS + 2)
                    dve.scalar_tensor_tensor(t_carry[:, :], t_dst[:, :], float(WIN), t_carry[:, :], op0=ALU.is_lt, op1=ALU.mult).then_inc(g_step, 1)
                    dve.wait_ge(g_step, w * GS + 3)
                    dve.scalar_tensor_tensor(t_key[:, :], t_key[:, :], 1.0, t_carry[:, :], op0=ALU.add, op1=ALU.mult).then_inc(g_step, 1)
                    dve.wait_ge(g_step, w * GS + 4)
                    dve.tensor_scalar(t_key[:, :], t_key[:, :], -1.0, None, ALU.add).then_inc(g_step, 1)
                    dve.tensor_scalar(t_dst[:, :], t_dst[:, :], float(-WIN), None, ALU.add).then_inc(g_step, 1)
                    wait_apart(dve, g_step, w * GS + 6)
                    with dve.Fori(0, TILES // RING) as i:
                        for half in range(2):
                            one_hots(i, half, w * TILES, g_used, g_onehots, False)
                dve.wait_ge(self_ready, 1)
                u_half(0, 0, 0, CW)
                u_half(0, 1, 0, CW)
            with dve.Else():
                def one_hot_loop(start, end, stats=0):
                    with dve.Fori(start, end) as i:
                        for half in range(2):
                            one_hots(i, half, 0, counts_done, onehots, True)
                        for n in range(stats):
                            s = bass.ds(LN_EARLY + stats * i + n, 1)
                            dve.bn_stats(ln_st[:, s, :], xs[:, s, :]).then_inc(ln_stat, 1)

                dve.tensor_scalar(oh_b[:, 0, :], iota_b[:, :], t_b[:, TILES - 2:TILES - 1], None, ALU.is_equal)
                dve.tensor_scalar(oh_carry[:, 0, :], iota_a[:, :], t_carry[:, TILES - 2:TILES - 1], None, ALU.is_equal).then_inc(seam_ready, 1)
                dve.wait_ge(seam_used, 1)
                one_hot_loop(0, LN_STEP, stats=(NT - LN_EARLY) // LN_STEP)
                ln_variance()
                one_hot_loop(LN_STEP, LN_STEP + 2)
                ln_scale_shift()
                one_hot_loop(LN_STEP + 2, X_READ)
                dve.wait_ge(feat_ready, 5)
                one_hot_loop(X_READ, EVAC_STEP)
                dve.wait_ge(self_ready, 1)
                u_half(0, 0, 0, CW)
                u_half(0, 1, 0, CW)
                one_hot_loop(EVAC_STEP, TILES // RING)

            dve.sem_inc(x1_done, QT)
            dve.sem_inc(stat_done[1], K1)

            dve.wait_ge(built, 1)
            dve.wait_ge(self_ready, 1)
            S0 = 4

            def x1_norm(c, q, p):
                dve.wait_ge(x_tile_in, 16 * c + 16)
                for t in range(q):
                    dve.wait_ge(lin[0], QT * c + t + 1 + QT)
                    dve.scalar_tensor_tensor(xt[0:p, t, :], ps[t][0:p, 0:D], 0.0, xt[0:p, t, :], op0=ALU.max, op1=ALU.add).then_inc(x1_done, 1)
                dve.wait_ge(x1_done, QT * c + q + QT)
                for t in range(q):
                    ins = dve.bn_stats(ln_st[0:p, t, :], xt[0:p, t, :])
                ins.then_inc(l0_step, 1)
                wait_apart(dve, l0_step, S0 * c + 1)
                for t in range(q):
                    ins = dve.bn_aggr(ln_mv[0:p, t, :], ln_st[0:p, t, :])
                ins.then_inc(l0_step, 1)
                dve.wait_ge(l0_step, S0 * c + 2)
                dve.tensor_scalar(ln_tmp[0:p, 0, 0:q], ln_mv[0:p, 0:q, 1], LN_EPS, None, ALU.add).then_inc(var0, 1)
                dve.wait_ge(sd0, c + 1)
                dve.reciprocal(ln_tmp[0:p, 2, 0:q], ln_tmp[0:p, 1, 0:q]).then_inc(l0_step, 1)
                dve.wait_ge(l0_step, S0 * c + 3)
                dve.tensor_scalar(ln_tmp[0:p, 2, 0:q], ln_tmp[0:p, 2, 0:q], SPLIT, None, ALU.mult).then_inc(l0_step, 1)
                dve.wait_ge(l0_step, S0 * c + 4)
                dve.scalar_tensor_tensor(ln_tmp[0:p, 3, 0:q], ln_mv[0:p, 0:q, 0], -1.0, ln_tmp[0:p, 2, 0:q], op0=ALU.mult, op1=ALU.mult).then_inc(norm0, 1)
                dve.wait_ge(hi0, c + 1)
                dve.tensor_tensor(hl[0:p, 0:q, D:2 * D], hp[0:p, 0:q, :], hl[0:p, 0:q, 0:D], ALU.subtract).then_inc(lo0, 1)

            u_half(0, 0, 1, CW)
            u_half(0, 1, 1, CW)
            x1_norm(0, QT, P)
            with dve.Fori(2, NC) as c:
                u_half(0, 0, c, CW)
                x1_norm(c - 1, QT, P)
                u_half(0, 1, c, CW)
            u_half(0, 0, NC, TW)
            u_half(0, 1, NC, TW)
            x1_norm(NC - 1, QT, P)
            dve.wait_ge(x1_out, 16 * (NC + 1))
            dve.memset(xt[0:TW, 0, :], 0.0).then_inc(tail_clear, 1)
            x1_norm(NC, 1, TW)

            def z_stats(l, c, w, ms, credit):
                for m in ms:
                    dve.wait_ge(z_out[l], credit + len_m[l] * c + m + 1)
                    if w == CW:
                        dve.bn_stats(stats[:, m, bass.ds(c, 1), :], z(m, c, w)).then_inc(stat_done[l], 1)
                    else:
                        tail = z(m, c, w)
                        dve.bn_stats(stats[:, m, NC, :], tail[:, 0, 0:TW // 2])
                        dve.bn_stats(stats[:, m, NC + 1, :], tail[:, 1, 0:REST - TW // 2]).then_inc(stat_done[l], 1)

            len_m = {1: K1, 2: K2, 3: K3}

            def bn_finish(l, m, credit):
                dve.wait_ge(stat_done[l], credit + m * (NC + 1))
                for t in range(m):
                    mark(dve.bn_aggr(bn_mv[:, t, :], stats[:, t, :, :].rearrange("p c s -> p (c s)")))
                sync()
                dve.tensor_scalar(bn_tmp[:, 0, 0:m], bn_mv[:, 0:m, 1], BN_EPS, None, ALU.add).then_inc(bn_var[l], 1)
                dve.wait_ge(bn_sd[l], 1)
                done(dve.reciprocal(bn_tmp[:, 2, 0:m], bn_tmp[:, 1, 0:m]))
                done(dve.tensor_tensor(bn_scale[:, 0:m], bn_tmp[:, 2, 0:m], gamma[l][:, 0:m], ALU.mult))
                done(dve.tensor_tensor(bn_tmp[:, 3, 0:m], bn_mv[:, 0:m, 0], bn_scale[:, 0:m], ALU.mult))
                dve.tensor_tensor(bn_shift[:, 0:m], beta[l][:, 0:m], bn_tmp[:, 3, 0:m], ALU.subtract).then_inc(bn_ready[l], 1)

            dve.wait_ge(feat_out, 16 * (NC + 2))
            u_half(1, 0, 0, CW)
            u_half(1, 1, 0, CW)
            with dve.Fori(1, NC) as c:
                u_half(1, 0, c, CW)
                z_stats(1, c - 1, CW, range(K1), K1)
                u_half(1, 1, c, CW)
            u_half(1, 0, NC, TW)
            z_stats(1, NC - 1, CW, range(K1), K1)
            u_half(1, 1, NC, TW)
            z_stats(1, NC, TW, range(K1), K1)
            dve.wait_ge(consts_in, 16 * 10)
            bn_finish(1, K1, K1)

            def elu(l, c, w, split_weights=False):
                K = KIN[l]
                for k in range(K):
                    if split_weights:
                        dve.wait_ge(w_hi[2], k + 1)
                        dve.tensor_tensor(lo_w[2][:, k, :], w2_first[:, :] if k == 0 else raw_w[2][:, k, :], hi_w[2][:, k, :],
                                          ALU.subtract).then_inc(w_lo[2], 1)
                    dve.wait_ge(er[l], K * c + k + 1)
                    dve.scalar_tensor_tensor(t_buf[:, k % 2, 0:w], e_buf[:, k % 2, 0:w], 1.0, r_buf[:, k % 2, 0:w],
                                             op0=ALU.min, op1=ALU.add).then_inc(er_used[l], 1)
                    dve.wait_ge(act_used[l], K * c + k + 1)
                    dve.wait_ge(er_used[l], K * c + k + 1 + 2)
                    if l == 4:
                        dve.tensor_scalar(act_in[:, k, 0:w], t_buf[:, k % 2, 0:w], -1.0, None, ALU.add).then_inc(act_ready[l], 1)
                    else:
                        hi = act_hi[:, k % SLOTS, 0:w]
                        dve.tensor_scalar(hi, t_buf[:, k % 2, 0:w], -1.0, None, ALU.add).then_inc(hi_ready[l], 1)
                        dve.wait_ge(hi_ready[l], K * c + k + 1)
                        dve.scalar_tensor_tensor(act_lo[:, k % SLOTS, 0:w], t_buf[:, k % 2, 0:w], -1.0, hi,
                                                 op0=ALU.add, op1=ALU.subtract).then_inc(act_ready[l], 1)

            for l in (2, 3, 4):
                dve.sem_inc(er_used[l], 2)
            dve.sem_inc(o_done, 2 * QT)
            HALF = K2 // 2
            elu(2, 0, CW, split_weights=True)
            with dve.Fori(0, NC - 1) as c:
                z_stats(2, c, CW, range(HALF), 8)
                elu(2, c + 1, CW)
                z_stats(2, c, CW, range(HALF, K2), 8)
            z_stats(2, NC - 1, CW, range(HALF), 8)
            elu(2, NC, TW)
            z_stats(2, NC - 1, CW, range(HALF, K2), 8)
            z_stats(2, NC, TW, range(K2), 8)
            bn_finish(2, K2, 0)

            elu(3, 0, CW)
            with dve.Fori(0, NC - 1) as c:
                elu(3, c + 1, CW)
                z_stats(3, c, CW, range(K3), 8)
            elu(3, NC, TW)
            z_stats(3, NC - 1, CW, range(K3), 8)
            z_stats(3, NC, TW, range(K3), 8)
            bn_finish(3, K3, 0)

            def add_x1(c, b, n, p, q):
                dve.wait_ge(x1_in[b], 16 * n + 16)
                dve.wait_ge(o_sent[b], 16 * n + 16)
                for t in range(q):
                    if t == q - 1:
                        dve.wait_ge(act_used[4], K3 * (c + 2))
                    else:
                        dve.wait_ge(prod[4], (QT - 1) * c + t + 1)
                    dve.tensor_tensor(ot[0:p, b, t, :], ps[4 * b + t][0:p, 0:D], x1t[0:p, b, t, :], ALU.add).then_inc(o_done, 1)

            elu(4, 0, CW)
            with dve.Fori(0, NC // 2 - 1) as j:
                for b in range(2):
                    elu(4, 2 * j + b + 1, CW)
                    add_x1(2 * j + b, b, j, P, QT)
            elu(4, NC - 1, CW)
            add_x1(NC - 2, 0, NC // 2 - 1, P, QT)
            elu(4, NC, TW)
            add_x1(NC - 1, 1, NC // 2 - 1, P, QT)
            add_x1(NC, 0, NC // 2, TW, 1)

        @block.tensor
        def _(pe):
            pe.wait_ge(pool_ready, POOL_SETUP)
            pe.wait_ge(nat_ready, 2)
            pe.wait_ge(lohi_ready, 2)
            for bank, row in ((0, AF), (1, BF), (2, DF)):
                for j in range(ET):
                    ins = pe.transpose(ps[bank][:, j * EP:(j + 1) * EP], edges(row)[:, j * P:(j + 1) * P], ident[0:EP, 0:EP])
                ins.then_inc(transposed, 1)

            pe.sem_inc(lin[0], QT)
            pe.sem_inc(lin[1], K1)
            pe.sem_inc(counts_done, RING)
            pe.sem_inc(g_used, RING)
            pe.wait_ge(tables_ready, 1)
            slow = pe.value_load(flag_i[0:1, 0:1])

            flat = feat[:, :, :].rearrange("p t d -> p (t d)")
            flat_counts = counts[:, :, :].rearrange("p t c -> p (t c)")

            def add_source(f, s, c, w=CW):
                for part in range(2):
                    pe.matmul(ps[6 + f][:, 0:w], flat[:, bass.ds(s * 2 * D + part * D + f * P, P)], flat_counts[:, bass.ds(s * AW + c * CW, w)],
                              start=(isinstance(s, int) and s == 0 and part == 0), stop=False, skip_group_check=True)

            def add_own(l, f, c, w):
                own = {0: ((0, ident16), (1, ident16)), 1: ((0, self_hi), (0, self_lo), (1, self_hi))}[l]
                for q in range(max(1, w // P)):
                    p = min(P, w)
                    for part, o in own:
                        ins = pe.matmul(ps[6 + f][:, q * P:q * P + p], flat[:, bass.ds((c * QT + q) * 2 * D + part * D + f * P, P)],
                                        o[:, 0:p], start=False, stop=True, skip_group_check=True)
                return ins

            def aggregate(l, f, c, w, first=False):
                pe.wait_ge(u_out[l], 2 * c + 1 + f)
                for s in range(NT):
                    if first and l == 1 and s % 6 == 0:
                        pe.wait_ge(feat_in[s // 6], 16)
                    add_source(f, s, c, w)
                add_own(l, f, c, w).then_inc(agg[l], 1)

            def open_bank(bank):
                pe.matmul(ps[bank][:, 0:KEYS], zero16[:, :], iota_key[:, :], start=True, stop=False, skip_group_check=True)

            with pe.If(slow > 0):
                with pe.Fori(0, NWIN) as w:
                    pe.wait_ge(g_window, w + 1)
                    open_bank(0)
                    with pe.Fori(0, TILES // RING) as i:
                        for t in range(RING):
                            pe.wait_ge(g_onehots, w * TILES + i * RING + t + 1)
                            pe.matmul(ps[0][:, 0:KEYS], oh_b[:, t, :], oh_key[:, t, :], start=False, stop=True,
                                      skip_group_check=True).then_inc(g_used, 1)
                pe.wait_ge(g_window, NWIN + 1)
                pe.wait_ge(feat_ready, 5)
                for c in EARLY:
                    for f in range(2):
                        aggregate(0, f, c, CW)
            with pe.Else():
                open_bank(0)
                open_bank(1)
                pe.wait_ge(seam_ready, 1)
                pe.matmul(ps[1][:, 0:KEYS:WIN], oh_b[:, 0, :], oh_carry[:, 0, :], start=False, stop=True,
                          skip_group_check=True).then_inc(seam_used, 1)

                def count_tiles(i, t0, count):
                    for t in range(t0, t0 + count):
                        if t % 2 == 0:
                            pe.wait_ge(onehots, i + t + 2)
                            pe.wait_ge(window_out, i + t + 4)
                        slot = t % RING
                        pe.matmul(ps[t % BANKS][:, 0:KEYS], oh_b[:, slot, :], oh_key[:, slot, :], start=False, stop=True,
                                  skip_group_check=True)
                        ins = pe.matmul(ps[(t + 2) % BANKS][:, 0:KEYS:WIN], oh_b[:, slot, :], oh_carry[:, slot, :], start=True, stop=False,
                                        skip_group_check=True)
                        if t % 2 == 1:
                            ins.then_inc(counts_done, 2)

                def count_and_add(c):
                    start, end, per_lap = EARLY[c]
                    pe.wait_ge(window_out, start * LAP + 4)
                    for f in range(2):
                        pe.wait_ge(u_out[0], 2 * c + 1 + f)
                        add_source(f, 0, c)
                    with pe.Fori(start, end) as lap:
                        adds = [(f, s + 1) for s in range(per_lap) for f in range(2)]
                        for t in range(0, LAP, 2):
                            count_tiles(lap * LAP, t, 2)
                            for f, s in adds[t * len(adds) // LAP:(t + 2) * len(adds) // LAP]:
                                add_source(f, (lap - start) * per_lap + s, c)

                def finish_chunk(c):
                    start, end, per_lap = EARLY[c]
                    for f in range(2):
                        for s in range((end - start) * per_lap + 1, NT):
                            add_source(f, s, c)
                        add_own(0, f, c, CW).then_inc(agg[0], 1)

                with pe.Fori(0, EARLY[0][0] * LAP, LAP) as i:
                    count_tiles(i, 0, LAP)
                pe.wait_ge(feat_ready, 5)
                count_and_add(0)
                finish_chunk(0)
                with pe.Fori(EARLY[0][1] * LAP, EARLY[1][0] * LAP, LAP) as i:
                    count_tiles(i, 0, LAP)
                count_and_add(1)
                count_tiles(LAPS * LAP, 0, TILES - LAPS * LAP)
                finish_chunk(1)
                pe.wait_ge(window_out, TILES + BANKS)
                pe.wait_ge(seam_back, 1)

            def linear0(c, w):
                pe.wait_ge(u_out[0], 2 * c + 4)
                for q in range(max(1, w // P)):
                    p = min(P, w)
                    pe.wait_ge(x1_done, QT * c + q + 1)
                    for k in range(DK):
                        ins = pe.matmul(ps[q][0:p, 0:D], u[:, k, q * P:q * P + p], w0[:, k, :], start=(k == 0), stop=(k == DK - 1))
                    ins.then_inc(lin[0], 1)

            def linear1(c, w):
                pe.wait_ge(u_out[1], 2 * c + 4)
                for m in range(K1):
                    pe.wait_ge(z_out[1], K1 * c + m + 1)
                    for k in range(DK):
                        for n, (wt, a) in enumerate(((w1_hi, u_hi), (w1_hi, u_lo), (w1_lo, u_hi))):
                            ins = pe.matmul(ps[m][:, 0:w], wt[:, k, m * P:(m + 1) * P], a[:, k, 0:w],
                                            start=(k == 0 and n == 0), stop=(k == DK - 1 and n == 2))
                    ins.then_inc(lin[1], 1)

            pe.sem_inc(built, 2)
            pe.wait_ge(consts_in, 16 * 10)
            for l, linear in ((0, linear0), (1, linear1)):
                if l == 1:
                    pe.wait_ge(self_ready, 1)
                    aggregate(l, 0, 0, CW, first=True)
                    aggregate(l, 1, 0, CW)
                    pe.wait_ge(w1_lo_ready, 1)
                else:
                    linear(0, CW)
                with pe.Fori(1 if l == 1 else len(EARLY), NC) as c:
                    aggregate(l, 0, c, CW)
                    linear(c - 1, CW)
                    aggregate(l, 1, c, CW)
                aggregate(l, 0, NC, TW)
                linear(NC - 1, CW)
                aggregate(l, 1, NC, TW)
                linear(NC, TW)

            def dense_chunk(l, c, w, ms, bank, first=False):
                K, M = KIN[l], MOUT[l]
                for k in range(K):
                    if first:
                        pe.wait_ge(w_lo[l], k + 1)
                    pe.wait_ge(act_ready[l], K * c + k + 1)
                    for m in ms:
                        if k == 0:
                            pe.wait_ge(z_out[l], M * c + m + 1)
                        cols = slice(m * P, (m + 1) * P)
                        for n, (wt, a) in enumerate(((hi_w, act_hi), (hi_w, act_lo), (lo_w, act_hi))):
                            ins = pe.matmul(ps[bank + m][:, 0:w], wt[l][:, k, cols], a[:, k % SLOTS, 0:w],
                                            start=(k == 0 and n == 0), stop=(k == K - 1 and n == 2))
                        if m == M - 1:
                            ins.then_inc(act_used[l], 1)
                        elif k == K - 1:
                            ins.then_inc(prod[l], 1)

            def out_chunk(c, w, b):
                K = K3
                q_n, p = max(1, w // P), min(P, w)
                for k in range(K):
                    pe.wait_ge(act_ready[4], K * c + k + 1)
                    for q in range(q_n):
                        if k == 0:
                            pe.wait_ge(o_done, QT * c + q + 1)
                        ins = pe.matmul(ps[4 * b + q][0:p, 0:D], act_in[:, k, q * P:q * P + p], w4[:, k, :], start=(k == 0), stop=(k == K - 1))
                        if q == q_n - 1:
                            ins.then_inc(act_used[4], 1)
                        elif k == K - 1:
                            ins.then_inc(prod[4], 1)

            for l in (2, 3, 4):
                pe.sem_inc(act_used[l], SLOTS)
            low, high = range(K2 // 2), range(K2 // 2, K2)
            dense_chunk(2, 0, CW, low, 0, first=True)
            dense_chunk(2, 0, CW, high, 0)
            with pe.Fori(1, NC) as c:
                dense_chunk(2, c, CW, low, 0)
                dense_chunk(2, c, CW, high, 0)
            dense_chunk(2, NC, TW, low, 0)
            dense_chunk(2, NC, TW, high, 0)
            dense_chunk(3, 0, CW, range(K3), 0, first=True)
            with pe.Fori(0, NC // 2 - 1) as j:
                for b in range(2):
                    dense_chunk(3, 2 * j + b + 1, CW, range(K3), 4 * (1 - b))
            dense_chunk(3, NC - 1, CW, range(K3), 4)
            dense_chunk(3, NC, TW, range(K3), 0)
            pe.wait_ge(w4_in, 16)
            with pe.Fori(0, NC // 2) as j:
                for b in range(2):
                    out_chunk(2 * j + b, CW, b)
            out_chunk(NC, TW, 0)


_INS = ['x', 'src', 'dst', 'L0_gnn_weight1', 'L1_gnn_eps', 'L1_gnn_W1', 'L1_gnn_b1', 'L1_gnn_g1', 'L1_gnn_beta1',
        'L1_gnn_W2', 'L1_gnn_b2', 'L1_gnn_g2', 'L1_gnn_beta2', 'L1_gnn_W3', 'L1_gnn_b3', 'L1_gnn_g3', 'L1_gnn_beta3',
        'L1_gnn_W4', 'L1_gnn_b4']


def kernel(**inputs):
    import numpy as _np
    import concourse.bacc as _bacc
    from concourse import mybir as _mybir
    from concourse.bass_utils import run_bass_kernel_spmd as _run

    nc = _bacc.Bacc("TRN2", target_bir_lowering=False, num_devices=1)
    arrays, args = {}, []
    for name in _INS:
        a = _np.ascontiguousarray(inputs[name])
        arrays[f"in_{name}_dram"] = a
        args.append(nc.dram_tensor(f"in_{name}_dram", a.shape, _mybir.dt.from_np(a.dtype), kind="ExternalInput").ap())
    args.append(nc.dram_tensor("out_0_dram", inputs["x"].shape, _mybir.dt.float32, kind="ExternalOutput").ap())
    gnn_two_layer_program(nc, *args)
    r = _run(nc, [arrays], core_ids=[0])
    return r.results[0]["out_0_dram"]
```
